# Optimizing a Trainium2 kernel written in Bass

```python
import numpy as np
import jax
import jax.numpy as jnp

def _softmax(x, axis=-1):
    return jax.nn.softmax(x, axis=axis)

def _gelu(x):
    return jax.nn.gelu(x, approximate=True)

def _silu(x):
    return jax.nn.silu(x)

def _sigmoid(x):
    return jax.nn.sigmoid(x)

def _layernorm(x, axis=-1, eps=1e-05):
    m = jnp.mean(x, axis=axis, keepdims=True)
    v = jnp.var(x, axis=axis, keepdims=True)
    return (x - m) / jnp.sqrt(v + eps)

def _scatter_add(tgt, idx, src, axis=0):
    return tgt.at[idx].add(src)

def _segment_sum(src, seg, n):
    return jax.ops.segment_sum(src, seg, n)
kernel_name = 'mk_gnn_preln_d4_gnn_r16_780088'

def setup_inputs(seed: int=0):
    np.random.seed(seed)
    _w = jnp.asarray

    def _rec_inputs():
        import jax
        import jax.numpy as jnp
        _gk = jax.random.key(seed)
        x = -0.0002117 + 1 * jax.random.normal(jax.random.fold_in(_gk, 1), (3125, 256), jnp.float32)
        src = jax.random.randint(jax.random.fold_in(_gk, 2), (50000,), 0, 3125, jnp.int32)
        dst = jax.random.randint(jax.random.fold_in(_gk, 3), (50000,), 0, 3125, jnp.int32)
        _o = jnp.argsort(dst, stable=True)
        src = src[_o]
        dst = dst[_o]
        edge_weight = jax.random.uniform(jax.random.fold_in(_gk, 13), (50000,), jnp.float32, 0.0, 1)
        return (x, src, dst, edge_weight)
    x, src, dst, edge_weight = _rec_inputs()

    def _L0_gnn_setup():
        import jax, jax.numpy as jnp
        import numpy as np
        N_NODES = 6250
        N_EDGES = 200000
        C = 256
        key = jax.random.key(seed)
        k1, k2, k3, k4 = jax.random.split(key, 4)
        x = jax.random.normal(k1, (N_NODES, C), dtype=jnp.float32)
        edge_weight = jax.random.uniform(k2, (N_EDGES,), dtype=jnp.float32)
        row = jax.random.randint(k3, (N_EDGES,), 0, N_NODES)
        col = jax.random.randint(k4, (N_EDGES,), 0, N_NODES)
        edge_index = jnp.stack([row, col]).astype(jnp.int64)
        return {'x': x, 'edge_weight': edge_weight, 'edge_index': edge_index}
    _L0_gnn_all = _L0_gnn_setup()
    _L0_gnn_in = {k: v for k, v in _L0_gnn_all.items() if k in ()}
    del _L0_gnn_all

    def _L1_gnn_setup():
        import jax, jax.numpy as jnp
        import numpy as np
        N_NODES = 1024
        N_EDGES = 16384
        D_IN = 256
        D = 256
        H = 512
        E = 64
        TOP_K = 2
        CAP = 1024
        BN_EPS = 1e-05

        def _moe_ff(x, Wg, bg, w1, b1, w2, b2):
            N = x.shape[0]
            logits = x @ Wg + bg
            vals, idx = jax.lax.top_k(logits, TOP_K)
            gates = jax.nn.softmax(vals, axis=-1)
            e_flat = idx.reshape(-1)
            g_flat = gates.reshape(-1)
            tok = jnp.arange(N * TOP_K) // TOP_K
            order = jnp.argsort(e_flat)
            e_s, tok_s, g_s = (e_flat[order], tok[order], g_flat[order])
            counts = jnp.bincount(e_flat, length=E)
            offs = jnp.concatenate([jnp.zeros((1,), counts.dtype), jnp.cumsum(counts)[:-1]])
            rank = jnp.arange(N * TOP_K) - offs[e_s]
            valid = rank < CAP
            slot = jnp.where(valid, e_s * CAP + rank, E * CAP)
            buf = jnp.zeros((E * CAP + 1, D), x.dtype).at[slot].set(x[tok_s])
            h = buf[:E * CAP].reshape(E, CAP, D)
            h1 = jax.nn.gelu(jnp.einsum('ecd,edh->ech', h, w1) + b1[:, None, :], approximate=False)
            h2 = jnp.einsum('ech,ehd->ecd', h1, w2) + b2[:, None, :]
            out_buf = h2.reshape(E * CAP, D)
            y_s = jnp.where(valid[:, None], out_buf[jnp.minimum(slot, E * CAP - 1)], 0.0)
            return jnp.zeros((N, D), x.dtype).at[tok_s].add(g_s[:, None] * y_s)

        def _forward(feats, W_gc, b_gc, W_res, b_res, Wg, bg, w1, b1, w2, b2, gamma, beta, src, dst):
            n = feats.shape[0]
            ones = jnp.ones((src.shape[0],), feats.dtype)
            deg_out = jnp.clip(jax.ops.segment_sum(ones, src, num_segments=n), 1.0)
            deg_in = jnp.clip(jax.ops.segment_sum(ones, dst, num_segments=n), 1.0)
            h = feats * jax.lax.rsqrt(deg_out)[:, None]
            m = jax.ops.segment_sum(h[src], dst, num_segments=n) * jax.lax.rsqrt(deg_in)[:, None]
            gc = m @ W_gc + b_gc
            x = gc + (feats @ W_res + b_res)
            core = _moe_ff(x, Wg, bg, w1, b1, w2, b2)
            y = x + core
            mean = jnp.mean(y, axis=0)
            var = jnp.mean((y - mean) ** 2, axis=0)
            return (y - mean) * jax.lax.rsqrt(var + BN_EPS) * gamma + beta
        key = jax.random.key(seed)
        ks = jax.random.split(key, 16)
        s = lambda d: 1.0 / np.sqrt(d)
        inp = {'feats': jax.random.normal(ks[0], (N_NODES, D_IN), jnp.float32), 'W_gc': jax.random.normal(ks[1], (D_IN, D), jnp.float32) * s(D_IN), 'b_gc': jnp.zeros((D,), jnp.float32), 'W_res': jax.random.normal(ks[2], (D_IN, D), jnp.float32) * s(D_IN), 'b_res': jnp.zeros((D,), jnp.float32), 'Wg': jax.random.normal(ks[3], (D, E), jnp.float32) * s(D), 'bg': jnp.zeros((E,), jnp.float32), 'w1': jax.random.normal(ks[4], (E, D, H), jnp.float32) * s(D), 'b1': jnp.zeros((E, H), jnp.float32), 'w2': jax.random.normal(ks[5], (E, H, D), jnp.float32) * s(H), 'b2': jnp.zeros((E, D), jnp.float32), 'gamma': jnp.ones((D,), jnp.float32), 'beta': jnp.zeros((D,), jnp.float32), 'src': jax.random.randint(ks[6], (N_EDGES,), 0, N_NODES), 'dst': jax.random.randint(ks[7], (N_EDGES,), 0, N_NODES)}
        return inp
    _L1_gnn_all = _L1_gnn_setup()
    _L1_gnn_in = {k: v for k, v in _L1_gnn_all.items() if k in ('W_gc', 'b_gc', 'W_res', 'b_res', 'Wg', 'bg', 'w1', 'b1', 'w2', 'b2', 'gamma', 'beta')}
    del _L1_gnn_all

    def _L2_gnn_setup():
        import jax, jax.numpy as jnp
        import numpy as np
        N_NODES = 625
        N_EDGES = 20000
        D_FEAT = 256
        N_LAYERS = 4
        EPS = 1e-16

        def _agnn_layer(h, src, dst, beta, num_nodes):
            h_norm = h * jax.lax.rsqrt(jnp.sum(h * h, axis=-1, keepdims=True) + EPS)
            cos = jnp.sum(h_norm[src] * h_norm[dst], axis=-1)
            logits = beta * cos
            m = jax.ops.segment_max(logits, dst, num_segments=num_nodes)
            ex = jnp.exp(logits - m[dst])
            denom = jax.ops.segment_sum(ex, dst, num_segments=num_nodes)
            alpha = ex / (denom[dst] + EPS)
            msg = alpha[:, None] * h[src]
            return jax.ops.segment_sum(msg, dst, num_segments=num_nodes)
        key = jax.random.key(seed)
        k1, k2, k3 = jax.random.split(key, 3)
        feats = jax.random.normal(k1, (N_NODES, D_FEAT), dtype=jnp.float32)
        src = jax.random.randint(k2, (N_EDGES,), 0, N_NODES, dtype=jnp.int32)
        dst = jax.random.randint(k3, (N_EDGES,), 0, N_NODES, dtype=jnp.int32)
        betas = jnp.ones((N_LAYERS,), dtype=jnp.float32)
        return {'feats': feats, 'src': src, 'dst': dst, 'betas': betas}
    _L2_gnn_all = _L2_gnn_setup()
    _L2_gnn_in = {k: v for k, v in _L2_gnn_all.items() if k in ('betas',)}
    del _L2_gnn_all

    def _L3_gnn_setup():
        import jax, jax.numpy as jnp
        import numpy as np
        N = 1250
        E = 20000
        HEADS = 4
        C = 64
        NEG_SLOPE = 0.2

        def _gat_layer(x, src, dst, W, a_s, a_d, b):
            n = x.shape[0]
            h = (x @ W).reshape(n, HEADS, C)
            s_src = jnp.einsum('nhc,hc->nh', h, a_s)
            s_dst = jnp.einsum('nhc,hc->nh', h, a_d)
            e = jax.nn.leaky_relu(s_src[src] + s_dst[dst], NEG_SLOPE)
            m = jax.ops.segment_max(e, dst, num_segments=n)
            ex = jnp.exp(e - m[dst])
            denom = jax.ops.segment_sum(ex, dst, num_segments=n)
            alpha = ex / denom[dst]
            msg = h[src] * alpha[:, :, None]
            out = jax.ops.segment_sum(msg, dst, num_segments=n)
            return out.reshape(n, HEADS * C) + b
        key = jax.random.key(seed)
        ks = jax.random.split(key, 16)
        x = jax.random.normal(ks[0], (N, 256), dtype=jnp.float32)
        edge_index = jax.random.randint(ks[1], (2, E), 0, N, dtype=jnp.int64)
        d = {'x': x, 'edge_index': edge_index}
        i = 2
        for l, fin in ((1, 256), (2, 256), (3, 256)):
            scale = 1.0 / np.sqrt(fin)
            d[f'W{l}'] = jax.random.normal(ks[i], (fin, HEADS * C), dtype=jnp.float32) * scale
            i += 1
            d[f'a_src{l}'] = jax.random.normal(ks[i], (HEADS, C), dtype=jnp.float32) * scale
            i += 1
            d[f'a_dst{l}'] = jax.random.normal(ks[i], (HEADS, C), dtype=jnp.float32) * scale
            i += 1
            d[f'b{l}'] = jnp.zeros((HEADS * C,), dtype=jnp.float32)
        return d
    _L3_gnn_all = _L3_gnn_setup()
    _L3_gnn_in = {k: v for k, v in _L3_gnn_all.items() if k in ('W1', 'a_src1', 'a_dst1', 'b1', 'W2', 'a_src2', 'a_dst2', 'b2', 'W3', 'a_src3', 'a_dst3', 'b3')}
    del _L3_gnn_all
    return {'x': x, 'src': src, 'dst': dst, 'edge_weight': edge_weight, 'L1_gnn_W_gc': _L1_gnn_in['W_gc'], 'L1_gnn_b_gc': _L1_gnn_in['b_gc'], 'L1_gnn_W_res': _L1_gnn_in['W_res'], 'L1_gnn_b_res': _L1_gnn_in['b_res'], 'L1_gnn_Wg': _L1_gnn_in['Wg'], 'L1_gnn_bg': _L1_gnn_in['bg'], 'L1_gnn_w1': _L1_gnn_in['w1'], 'L1_gnn_b1': _L1_gnn_in['b1'], 'L1_gnn_w2': _L1_gnn_in['w2'], 'L1_gnn_b2': _L1_gnn_in['b2'], 'L1_gnn_gamma': _L1_gnn_in['gamma'], 'L1_gnn_beta': _L1_gnn_in['beta'], 'L2_gnn_betas': _L2_gnn_in['betas'], 'L3_gnn_W1': _L3_gnn_in['W1'], 'L3_gnn_a_src1': _L3_gnn_in['a_src1'], 'L3_gnn_a_dst1': _L3_gnn_in['a_dst1'], 'L3_gnn_b1': _L3_gnn_in['b1'], 'L3_gnn_W2': _L3_gnn_in['W2'], 'L3_gnn_a_src2': _L3_gnn_in['a_src2'], 'L3_gnn_a_dst2': _L3_gnn_in['a_dst2'], 'L3_gnn_b2': _L3_gnn_in['b2'], 'L3_gnn_W3': _L3_gnn_in['W3'], 'L3_gnn_a_src3': _L3_gnn_in['a_src3'], 'L3_gnn_a_dst3': _L3_gnn_in['a_dst3'], 'L3_gnn_b3': _L3_gnn_in['b3']}

def reference(x, src, dst, edge_weight, L1_gnn_W_gc, L1_gnn_b_gc, L1_gnn_W_res, L1_gnn_b_res, L1_gnn_Wg, L1_gnn_bg, L1_gnn_w1, L1_gnn_b1, L1_gnn_w2, L1_gnn_b2, L1_gnn_gamma, L1_gnn_beta, L2_gnn_betas, L3_gnn_W1, L3_gnn_a_src1, L3_gnn_a_dst1, L3_gnn_b1, L3_gnn_W2, L3_gnn_a_src2, L3_gnn_a_dst2, L3_gnn_b2, L3_gnn_W3, L3_gnn_a_src3, L3_gnn_a_dst3, L3_gnn_b3):
    import jax
    import jax.numpy as jnp

    def _L0_gnn_ref(x, edge_weight, edge_index):
        import jax, jax.numpy as jnp
        import numpy as np
        N_NODES = 6250
        N_EDGES = 200000
        C = 256
        n = x.shape[0]
        c_half = x.shape[-1] // 2
        row, col = (edge_index[0], edge_index[1])
        ones = jnp.ones(edge_index.shape[1], dtype=x.dtype)
        deg_row = jax.ops.segment_sum(ones, row, num_segments=n)
        deg_col = jax.ops.segment_sum(ones, col, num_segments=n)
        w = edge_weight[:, None]
        msg_fwd = w * x[col, :c_half]
        x_fwd = jax.ops.segment_sum(msg_fwd, row, num_segments=n)
        x_fwd = x_fwd / jnp.clip(deg_row, 1.0)[:, None]
        msg_bwd = w * x[row, c_half:]
        x_bwd = jax.ops.segment_sum(msg_bwd, col, num_segments=n)
        x_bwd = x_bwd / jnp.clip(deg_col, 1.0)[:, None]
        return jnp.concatenate([x_fwd, x_bwd], axis=-1)

    def _L1_gnn_ref(feats, W_gc, b_gc, W_res, b_res, Wg, bg, w1, b1, w2, b2, gamma, beta, src, dst):
        import jax, jax.numpy as jnp
        import numpy as np
        N_NODES = 1024
        N_EDGES = 16384
        D_IN = 256
        D = 256
        H = 512
        E = 64
        TOP_K = 2
        CAP = 1024
        BN_EPS = 1e-05

        def _moe_ff(x, Wg, bg, w1, b1, w2, b2):
            N = x.shape[0]
            logits = x @ Wg + bg
            vals, idx = jax.lax.top_k(logits, TOP_K)
            gates = jax.nn.softmax(vals, axis=-1)
            e_flat = idx.reshape(-1)
            g_flat = gates.reshape(-1)
            tok = jnp.arange(N * TOP_K) // TOP_K
            order = jnp.argsort(e_flat)
            e_s, tok_s, g_s = (e_flat[order], tok[order], g_flat[order])
            counts = jnp.bincount(e_flat, length=E)
            offs = jnp.concatenate([jnp.zeros((1,), counts.dtype), jnp.cumsum(counts)[:-1]])
            rank = jnp.arange(N * TOP_K) - offs[e_s]
            valid = rank < CAP
            slot = jnp.where(valid, e_s * CAP + rank, E * CAP)
            buf = jnp.zeros((E * CAP + 1, D), x.dtype).at[slot].set(x[tok_s])
            h = buf[:E * CAP].reshape(E, CAP, D)
            h1 = jax.nn.gelu(jnp.einsum('ecd,edh->ech', h, w1) + b1[:, None, :], approximate=False)
            h2 = jnp.einsum('ech,ehd->ecd', h1, w2) + b2[:, None, :]
            out_buf = h2.reshape(E * CAP, D)
            y_s = jnp.where(valid[:, None], out_buf[jnp.minimum(slot, E * CAP - 1)], 0.0)
            return jnp.zeros((N, D), x.dtype).at[tok_s].add(g_s[:, None] * y_s)

        def _forward(feats, W_gc, b_gc, W_res, b_res, Wg, bg, w1, b1, w2, b2, gamma, beta, src, dst):
            n = feats.shape[0]
            ones = jnp.ones((src.shape[0],), feats.dtype)
            deg_out = jnp.clip(jax.ops.segment_sum(ones, src, num_segments=n), 1.0)
            deg_in = jnp.clip(jax.ops.segment_sum(ones, dst, num_segments=n), 1.0)
            h = feats * jax.lax.rsqrt(deg_out)[:, None]
            m = jax.ops.segment_sum(h[src], dst, num_segments=n) * jax.lax.rsqrt(deg_in)[:, None]
            gc = m @ W_gc + b_gc
            x = gc + (feats @ W_res + b_res)
            core = _moe_ff(x, Wg, bg, w1, b1, w2, b2)
            y = x + core
            mean = jnp.mean(y, axis=0)
            var = jnp.mean((y - mean) ** 2, axis=0)
            return (y - mean) * jax.lax.rsqrt(var + BN_EPS) * gamma + beta
        return _forward(feats, W_gc, b_gc, W_res, b_res, Wg, bg, w1, b1, w2, b2, gamma, beta, src, dst)

    def _L2_gnn_ref(feats, src, dst, betas):
        import jax, jax.numpy as jnp
        import numpy as np
        N_NODES = 625
        N_EDGES = 20000
        D_FEAT = 256
        N_LAYERS = 4
        EPS = 1e-16

        def _agnn_layer(h, src, dst, beta, num_nodes):
            h_norm = h * jax.lax.rsqrt(jnp.sum(h * h, axis=-1, keepdims=True) + EPS)
            cos = jnp.sum(h_norm[src] * h_norm[dst], axis=-1)
            logits = beta * cos
            m = jax.ops.segment_max(logits, dst, num_segments=num_nodes)
            ex = jnp.exp(logits - m[dst])
            denom = jax.ops.segment_sum(ex, dst, num_segments=num_nodes)
            alpha = ex / (denom[dst] + EPS)
            msg = alpha[:, None] * h[src]
            return jax.ops.segment_sum(msg, dst, num_segments=num_nodes)
        h = feats
        num_nodes = feats.shape[0]
        for i in range(N_LAYERS):
            h = _agnn_layer(h, src, dst, betas[i], num_nodes)
            h = jax.nn.relu(h)
        return h

    def _L3_gnn_ref(x, edge_index, W1, a_src1, a_dst1, b1, W2, a_src2, a_dst2, b2, W3, a_src3, a_dst3, b3):
        import jax, jax.numpy as jnp
        import numpy as np
        N = 1250
        E = 20000
        HEADS = 4
        C = 64
        NEG_SLOPE = 0.2

        def _gat_layer(x, src, dst, W, a_s, a_d, b):
            n = x.shape[0]
            h = (x @ W).reshape(n, HEADS, C)
            s_src = jnp.einsum('nhc,hc->nh', h, a_s)
            s_dst = jnp.einsum('nhc,hc->nh', h, a_d)
            e = jax.nn.leaky_relu(s_src[src] + s_dst[dst], NEG_SLOPE)
            m = jax.ops.segment_max(e, dst, num_segments=n)
            ex = jnp.exp(e - m[dst])
            denom = jax.ops.segment_sum(ex, dst, num_segments=n)
            alpha = ex / denom[dst]
            msg = h[src] * alpha[:, :, None]
            out = jax.ops.segment_sum(msg, dst, num_segments=n)
            return out.reshape(n, HEADS * C) + b
        loops = jnp.arange(N, dtype=edge_index.dtype)
        src = jnp.concatenate([edge_index[0], loops])
        dst = jnp.concatenate([edge_index[1], loops])
        h = _gat_layer(x, src, dst, W1, a_src1, a_dst1, b1)
        h = jax.nn.relu(h)
        h = _gat_layer(h, src, dst, W2, a_src2, a_dst2, b2)
        h = jax.nn.relu(h)
        h = _gat_layer(h, src, dst, W3, a_src3, a_dst3, b3)
        norm = jnp.maximum(jnp.linalg.norm(h, axis=-1, keepdims=True), 1e-12)
        return h / norm
    edge_index = jnp.stack([src, dst])
    h = jnp.maximum(_layernorm(x, axis=-1), 0.0)
    x = x + _L0_gnn_ref(h, edge_weight, edge_index)
    h = jnp.maximum(_layernorm(x, axis=-1), 0.0)
    x = x + _L1_gnn_ref(h, L1_gnn_W_gc, L1_gnn_b_gc, L1_gnn_W_res, L1_gnn_b_res, L1_gnn_Wg, L1_gnn_bg, L1_gnn_w1, L1_gnn_b1, L1_gnn_w2, L1_gnn_b2, L1_gnn_gamma, L1_gnn_beta, src, dst)
    h = jnp.maximum(_layernorm(x, axis=-1), 0.0)
    x = x + _L2_gnn_ref(h, src, dst, L2_gnn_betas)
    h = jnp.maximum(_layernorm(x, axis=-1), 0.0)
    x = x + _L3_gnn_ref(h, edge_index, L3_gnn_W1, L3_gnn_a_src1, L3_gnn_a_dst1, L3_gnn_b1, L3_gnn_W2, L3_gnn_a_src2, L3_gnn_a_dst2, L3_gnn_b2, L3_gnn_W3, L3_gnn_a_src3, L3_gnn_a_dst3, L3_gnn_b3)
    return x

_drawn_inputs = setup_inputs


def setup_inputs(seed=0):
    import zlib

    import numpy as np

    out = dict(_drawn_inputs(seed))
    spreads = {'L1_gnn_b_gc': (0.0, 0.1),
     'L1_gnn_b_res': (0.0, 0.1),
     'L1_gnn_bg': (0.0, 0.1),
     'L1_gnn_b1': (0.0, 0.1),
     'L1_gnn_b2': (0.0, 0.1),
     'L1_gnn_gamma': (1.0, 0.2),
     'L1_gnn_beta': (0.0, 0.1),
     'L2_gnn_betas': (1.0, 0.6),
     'L3_gnn_b1': (0.0, 2.0),
     'L3_gnn_b2': (0.0, 2.0),
     'L3_gnn_b3': (0.0, 1.502)}
    factors = {'L3_gnn_a_src1': 64.0,
     'L3_gnn_a_dst1': 64.0,
     'L3_gnn_a_src2': 64.0,
     'L3_gnn_a_dst2': 64.0,
     'L3_gnn_a_src3': 64.0,
     'L3_gnn_a_dst3': 64.0,
     'L3_gnn_W1': 7.203,
     'L3_gnn_W2': 2.823}
    for name, (base, spread) in spreads.items():
        noise = np.random.default_rng([zlib.crc32(name.encode()), seed]).standard_normal(out[name].shape)
        drawn = base * np.exp(spread * noise) if base else spread * noise
        out[name] = jnp.asarray(drawn.astype(out[name].dtype))
    for name, factor in factors.items():
        out[name] = (out[name] * factor).astype(out[name].dtype)
    return out
```

```python
from contextlib import ExitStack

import concourse.bass as bass
from concourse import mybir

ALU = mybir.AluOpType
ACT = mybir.ActivationFunctionType
AX = mybir.AxisListType
F32 = mybir.dt.float32
BF16 = mybir.dt.bfloat16
I32 = mybir.dt.int32
U32 = mybir.dt.uint32
ds = bass.ds

P = 128
N = 3125
NB = -(-N // P)
NP = NB * P
LAST = N - (NB - 1) * P
D = 256
DH = D // 2
E = 50000
J = -(-E // P)
J += -J % 4
TAIL = E - (P - 1) * J
G = 4
GE = G * P
U = 4
NG = (E + NB * (GE - 1)) // GE
NG += -NG % U
NI = NG // U
T = NG * G
NOWHERE = 200.0
BIG = 1.0e30
LN_EPS = 1e-5
W_AGNN = 260
HEADS = 4
C_HEAD = D // HEADS
CH1 = C_HEAD + 1
W_GAT = HEADS * CH1
PARTS = 3 * HEADS
W_ROW = W_GAT + PARTS // 2
L2_LAYERS = 4
L3_LAYERS = 3
NEG_SLOPE = 0.2
LOOPS = 1250
LB = -(-LOOPS // P)

EXPERTS = 64
HID = 512
TOP_K = 2
CAP = 1024
MT = (N * TOP_K + EXPERTS * (P - 1)) // P
MT += -MT % U
BN_EPS = 1e-5


def tagged(nc, name):
    return f"{name}_{nc.next_id()}"


class Shared:
    pass


class Chain:

    def __init__(self, eng, sem, base=0):
        self.eng, self.sem, self.base, self.n = eng, sem, base, 0

    def mark(self, ins):
        self.n += 1
        ins.then_inc(self.sem, 1)
        return ins

    def done(self, ins):
        self.mark(ins)
        self.eng.wait_ge(self.sem, self.base + self.n)


def pick(tile, i, *rest):
    return tile[(slice(None), ds(i, 1)) + rest]


def lagged(i, j, lag, total=NG):
    j2 = j - lag
    i2 = i
    while j2 < 0:
        i2, j2 = i2 - 1, j2 + U
    t = i2 * U + j2
    if isinstance(t, int) and not 0 <= t < total:
        return None
    return i2, j2, t


def pipeline(eng, step, drain, total=NG, numbers=None):
    if numbers:
        numbers.load(0)
    for j in range(U):
        step(0, j)
    with eng.Fori(1, total // U) as i:
        if numbers:
            numbers.load(i)
        for j in range(U):
            step(i, j)
    if numbers and drain:
        numbers.load(total // U)
    for j in range(drain):
        step(total // U, j)
    if numbers:
        numbers.free()


class Numbers:

    def __init__(self, nc, eng, table, name, top=NB - 1):
        self.eng, self.table, self.top = eng, table, top
        self.regs = [eng.alloc_register(tagged(nc, f"{name}{n}_")) for n in range(2 * U)]

    def load(self, i):
        self.eng.load(self.regs, self.table[:, ds(i * U, 2 * U)])

    def at(self, j, lag):
        return self.eng.snap(self.regs[U + j - lag], min_val=0, max_val=self.top)

    def free(self):
        for r in self.regs:
            self.eng.free_register(r)


def rows(dram):
    return dram.rearrange("(b p) c -> p b c", p=P)


def b3(ap, n):
    return ap.unsqueeze(2).to_broadcast([ap.shape[0], ap.shape[1], n])


def mid(ap, n):
    return ap.unsqueeze(1).to_broadcast([ap.shape[0], n, ap.shape[1]])


def load_inputs(nc, k, a):
    with ExitStack() as ctx:
        sem = lambda n: ctx.enter_context(nc.semaphore(tagged(nc, n)))
        s_clear = sem("s_clear")
        s_iota = sem("s_iota")
        s_const = sem("s_const")
        s_in = sem("s_in")
        s_pad = sem("s_pad")
        s_padout = sem("s_padout")
        padrec = ctx.enter_context(nc.sbuf_tensor(tagged(nc, "padrec"), [P, T, 4], I32))
        pcol = k.pcol
        with nc.Block() as block:

            @block.vector
            def _(dve):
                nc.vector.memset(k.X[:, NB - 1, :], 0.0).then_inc(s_clear, 1)
                nc.vector.memset(k.keys[:, :, :], NP).then_inc(s_clear, 1)
                nc.vector.memset(k.wts[:, :], 0.0).then_inc(s_clear, 1)
                nc.vector.memset(padrec[:, :, :], 0).then_inc(s_pad, 1)
                dve.wait_ge(s_pad, 1)
                nc.vector.memset(padrec[:, :, 1:2].bitcast(F32), NOWHERE).then_inc(s_pad, 1)
                nc.vector.memset(k.ones[:, :], 1.0)
                nc.vector.memset(k.zero[:, :], 0.0)
                dve.wait_ge(s_iota, 2)
                nc.vector.tensor_scalar(k.ident[:, :], k.iota[:, :], pcol[:, 0:1], None, ALU.is_equal).then_inc(s_const, 1)
                nc.vector.tensor_scalar(k.identb[:, :], k.iota[:, :], pcol[:, 0:1], None, ALU.is_equal).then_inc(s_const, 1)
                nc.vector.tensor_scalar(k.tri[:, :], k.iota[:, :], pcol[:, 0:1], None, ALU.is_gt).then_inc(s_const, 1)

            @block.gpsimd
            def _(pool):
                nc.gpsimd.iota(k.iota[:, :], [[1, P]], base=0, channel_multiplier=0,
                               allow_small_or_imprecise_dtypes=True).then_inc(s_iota, 1)
                nc.gpsimd.iota(pcol[:, :], [[0, 1]], base=0, channel_multiplier=1,
                               allow_small_or_imprecise_dtypes=True).then_inc(s_iota, 1)

            @block.sync
            def _(sp):
                sp.dma_start(k.X[:, 0:NB - 1, :], rows(a["x"][0:(NB - 1) * P, :])).then_inc(s_in, 16)
                sp.wait_ge(s_clear, 3)
                sp.dma_start(k.X[0:LAST, NB - 1, :], a["x"][(NB - 1) * P:N, :]).then_inc(s_in, 16)
                for n, key in enumerate((a["dst"], a["src"])):
                    sp.dma_start(k.keys[0:P - 1, n, :], key[0:(P - 1) * J].rearrange("(p j) -> p j", j=J)).then_inc(s_in, 16)
                    sp.dma_start(k.keys[P - 1:P, n, 0:TAIL], key[(P - 1) * J:E].unsqueeze(0)).then_inc(s_in, 16)
                sp.dma_start(k.wts[0:P - 1, :], a["edge_weight"][0:(P - 1) * J].rearrange("(p j) -> p j", j=J)).then_inc(s_in, 16)
                sp.dma_start(k.wts[P - 1:P, 0:TAIL], a["edge_weight"][(P - 1) * J:E].unsqueeze(0)).then_inc(s_in, 16)
                sp.wait_ge(s_pad, 2)
                for n in range(2):
                    sp.dma_start(k.rec_d[n, :, :, :], padrec[:, :, :]).then_inc(s_padout, 16)
                sp.wait_ge(s_in, 8 * 16)
                sp.wait_ge(s_padout, 2 * 16)


def sort_edges(nc, k):
    NK = NB + 1
    with ExitStack() as ctx:
        sb = lambda n, s, d: ctx.enter_context(nc.sbuf_tensor(tagged(nc, n), s, d))
        sem = lambda n: ctx.enter_context(nc.semaphore(tagged(nc, n)))
        s_chain = sem("s_chain")
        s_cnt = sem("s_cnt")
        s_tot = sem("s_tot")
        s_gb = sem("s_gb")
        s_gbd = sem("s_gbd")
        blk_i = sb("blk_i", [P, 2, J], I32)
        blk = sb("blk", [P, 2, J], F32)
        loc_i = sb("loc_i", [P, 2, J], I32)
        loc = sb("loc", [P, 2, J], F32)
        mask = sb("mask", [P, NK, 2, J], BF16)
        cnt = sb("cnt", [P, NK, 2], F32)
        bnum = sb("bnum", [P, NK], F32)
        scan = sb("scan", [P, 2, J], F32)
        pos = sb("pos", [P, 2, J], F32)
        onesj = sb("onesj", [P, J], F32)
        gi = sb("gi", [P, 2, NK], I32)
        gf = sb("gf", [P, 2, NK], F32)
        gend = sb("gend", [P, 2, NK], F32)
        offs = sb("offs", [P, 2, NK], F32)
        gb_f = sb("gb_f", [P, 2], F32)
        gb_i = sb("gb_i", [P, 2], I32)
        pos_i = sb("pos_i", [P, 2, J], I32)
        tile_i = sb("tile_i", [P, 2, J], I32)
        R = sb("R", [P, 2, J, 5], I32)
        slot = sb("slot", [P, 2, G, 5], I32)
        pref = ctx.enter_context(nc.psum_tensor(tagged(nc, "pref"), [P, NK * 2], F32))
        tot = ctx.enter_context(nc.psum_tensor(tagged(nc, "tot"), [P, NK * 2], F32))
        le = sb("le", [P, 2, NB], F32)

        with nc.Block() as block:

            @block.gpsimd
            def _(pool):
                nc.gpsimd.iota(bnum[:, :], [[1, NK]], base=0, channel_multiplier=0,
                               allow_small_or_imprecise_dtypes=True).then_inc(s_cnt, 1)

            @block.vector
            def _(dve):
                c = Chain(dve, s_chain)
                nc.vector.memset(onesj[:, :], 1.0)
                nc.vector.memset(k.gb[:, :, 0:U], 0)
                nc.vector.memset(k.gb[:, :, U + P:], 0)
                nc.vector.memset(pos[:, :, :], -1.0)
                c.mark(nc.vector.tensor_scalar(blk_i[:, :, :], k.keys[:, :, :], 7, None, ALU.arith_shift_right))
                c.done(nc.vector.tensor_scalar(loc_i[:, :, :], k.keys[:, :, :], P - 1, None, ALU.bitwise_and))
                c.mark(nc.vector.tensor_copy(blk[:, :, :], blk_i[:, :, :]))
                c.done(nc.vector.tensor_copy(loc[:, :, :], loc_i[:, :, :]))
                dve.wait_ge(s_cnt, 1)
                with dve.Fori(0, NK) as b:
                    nc.vector.tensor_scalar(pick(mask, b, slice(None), slice(None)).rearrange("p a k j -> p (a k j)"),
                                            blk[:, :, :].rearrange("p k j -> p (k j)"),
                                            pick(bnum, b), None, ALU.is_equal).then_inc(s_cnt, 1)
                dve.wait_ge(s_cnt, NK + 1)
                nc.vector.tensor_reduce(cnt[:, :, :], mask[:, :, :, :], AX.X, ALU.add).then_inc(s_cnt, 1)
                c.done(nc.vector.scalar_tensor_tensor(out=loc[:, :, :], in0=mask[:, NB, :, :], scalar=NOWHERE,
                                                      in1=loc[:, :, :], op0=ALU.mult, op1=ALU.add))
                dve.wait_ge(s_tot, 1)
                totv = tot[:, :].rearrange("p (b k) -> p k b", k=2)
                prefv = pref[:, :].rearrange("p (b k) -> p k b", k=2)
                c.done(nc.vector.tensor_scalar(gi[:, :, :], totv, float(GE - 1), None, ALU.add))
                c.done(nc.vector.tensor_scalar(gi[:, :, :], gi[:, :, :], GE.bit_length() - 1, None, ALU.arith_shift_right))
                c.done(nc.vector.tensor_copy(gf[:, :, :], gi[:, :, :]))
                for n in range(2):
                    c.mark(nc.vector.tensor_tensor_scan(gend[:, n, :], onesj[:, 0:NK], gf[:, n, :], 0.0, ALU.mult, ALU.add))
                dve.wait_ge(s_chain, c.n)
                c.done(nc.vector.tensor_tensor(gf[:, :, :], gend[:, :, :], gf[:, :, :], ALU.subtract))
                c.done(nc.vector.scalar_tensor_tensor(out=offs[:, :, :], in0=gf[:, :, :], scalar=float(GE), in1=prefv,
                                                      op0=ALU.mult, op1=ALU.add))
                for n in range(2):
                    c.mark(nc.vector.tensor_scalar(le[:, n, :], gend[:, n, 0:NB], k.pcol[:, 0:1], None, ALU.is_le))
                dve.wait_ge(s_chain, c.n)
                c.done(nc.vector.tensor_reduce(gb_f[:, :], le[:, :, :], AX.X, ALU.add))
                nc.vector.tensor_scalar(gb_i[:, :], gb_f[:, :], float(NB - 1), None, ALU.min).then_inc(s_gb, 1)
                base = c.n
                with dve.Fori(0, NK) as b:
                    c = Chain(dve, s_chain, base + b * 4)
                    m = pick(mask, b, slice(None), slice(None)).rearrange("p a k j -> p (a k) j")
                    for n in range(2):
                        c.mark(nc.vector.tensor_tensor_scan(scan[:, n, :], onesj[:, :],
                                                            pick(mask, b, n, slice(None)).rearrange("p a j -> p (a j)"),
                                                            offs[:, n, ds(b, 1)], ALU.mult, ALU.add))
                    dve.wait_ge(s_chain, c.base + c.n)
                    c.done(nc.vector.tensor_tensor(scan[:, :, :], scan[:, :, :], m, ALU.mult))
                    c.done(nc.vector.tensor_tensor(pos[:, :, :], pos[:, :, :], scan[:, :, :], ALU.add))
                c = Chain(dve, s_chain)
                c.n = base + NK * 4
                c.done(nc.vector.tensor_copy(pos_i[:, :, :], pos[:, :, :]))
                c.mark(nc.vector.tensor_scalar(tile_i[:, :, :], pos_i[:, :, :], 7, None, ALU.arith_shift_right))
                c.done(nc.vector.tensor_scalar(pos_i[:, :, :], pos_i[:, :, :], P - 1, None, ALU.bitwise_and))
                for n in range(2):
                    c.mark(nc.vector.tensor_scalar(pos[:, n, :], pos_i[:, n, :], float(T), float(n * P * T), ALU.mult, ALU.add))
                dve.wait_ge(s_chain, c.n)
                c.mark(nc.vector.tensor_tensor(R[:, :, :, 4], pos[:, :, :], tile_i[:, :, :], ALU.add))
                for n in range(2):
                    c.mark(nc.vector.tensor_scalar(R[:, n, :, 0], k.keys[:, 1 - n, :], float(NP - 1), None, ALU.min))
                    c.mark(nc.vector.tensor_copy(R[:, n, :, 2].bitcast(F32), k.wts[:, :]))
                    c.mark(nc.vector.memset(R[:, n, :, 3], 0))
                c.mark(nc.vector.tensor_copy(R[:, :, :, 1].bitcast(F32), loc[:, :, :]))
                dve.wait_ge(s_chain, c.n)

            @block.tensor
            def _(pe):
                pe.wait_ge(s_cnt, NK + 2)
                c2 = cnt[:, :, :].rearrange("p b k -> p (b k)")
                nc.tensor.matmul(pref[:, :], k.tri[:, :], c2, start=True, stop=True)
                nc.tensor.matmul(tot[:, :], k.ones[:, 0:P], c2, start=True, stop=True).then_inc(s_tot, 1)

            @block.sync
            def _(sp):
                sp.wait_ge(s_gb, 1)
                for n in range(2):
                    sp.dma_start(k.gb_d[n, :, :], gb_i[:, n:n + 1]).then_inc(s_gbd, 16)
                sp.wait_ge(s_gbd, 32)
                for n in range(2):
                    sp.dma_start(k.gb[:, n, U:U + P], k.gb_d[n, :, :].rearrange("g k -> k g")).then_inc(s_gbd, 16)
                sp.wait_ge(s_gbd, 64)

        s_slot = [sem(f"s_slot{n}") for n in range(2)]
        s_sent = [sem(f"s_sent{n}") for n in range(2)]
        s_gate = sem("s_gate")
        Rf = R[:, :, :, :].rearrange("p k j c -> p (k j c)")
        STEPS = 2 * J // (2 * G)
        s_zero = sem("s_zero")
        s_zeroed = sem("s_zeroed")
        with nc.Block() as block:

            @block.vector
            def _(dve):
                nc.vector.memset(k.acc[:, :, :], 0.0).then_inc(s_zero, 1)
                with dve.Fori(0, STEPS) as i:
                    for n in range(2):
                        dve.wait_ge(s_sent[n], i * (16 * G))
                        nc.vector.tensor_copy(slot[:, n, :, :].rearrange("p g c -> p (g c)"),
                                              Rf[:, ds((i * 2 + n) * (G * 5), G * 5)]).then_inc(s_slot[n], 1)

            @block.sync
            def _(sp):
                sp.wait_ge(s_zero, 1)
                for t in range(0, MT, NB):
                    n = min(NB, MT - t)
                    sp.dma_start(rows(k.xbuf[t * P:(t + n) * P, :]), k.acc[:, 0:n, 0:D]).then_inc(s_zeroed, 16)
                sp.wait_ge(s_zeroed, -(-MT // NB) * 16)

            @block.gpsimd
            def _(pool):
                with pool.Fori(0, STEPS) as i:
                    for n in range(2):
                        pool.wait_ge(s_slot[n], i + 1)
                        pool.sem_inc(s_gate, 1)
                        for g in range(G):
                            nc.gpsimd.indirect_dma_start(
                                out=k.rec_rows, out_offset=bass.IndirectOffsetOnAxis(ap=slot[:, n, g, 4:5], axis=0),
                                in_=slot[:, n, g, 0:4], in_offset=None).then_inc(s_sent[n], 16)
                for n in range(2):
                    pool.wait_ge(s_sent[n], STEPS * 16 * G)


def layernorm(nc, k, write):
    with ExitStack() as ctx:
        sb = lambda n, s, d: ctx.enter_context(nc.sbuf_tensor(tagged(nc, n), s, d))
        q = k.sems
        n = k.norms
        k.norms += 1
        sq = sb("sq", [P, NB, D], F32)
        mean = sb("mean", [P, NB], F32)
        var = sb("var", [P, NB], F32)
        rstd = sb("rstd", [P, NB], F32)
        with nc.Block() as block:

            @block.vector
            def _(dve):
                c = Chain(dve, q.ln, n * 6)
                Hf = k.H[:, :, 0:D]
                c.done(nc.vector.tensor_reduce(mean[:, :], k.X[:, :, :], AX.X, ALU.add))
                c.done(nc.vector.tensor_scalar(mean[:, :], mean[:, :], 1.0 / D, None, ALU.mult))
                c.done(nc.vector.tensor_tensor(Hf, k.X[:, :, :], b3(mean[:, :], D), ALU.subtract))
                dve.wait_ge(q.ln_sq, n + 1)
                c.done(nc.vector.tensor_reduce(var[:, :], sq[:, :, :], AX.X, ALU.add))
                c.done(nc.vector.tensor_scalar(var[:, :], var[:, :], 1.0 / D, LN_EPS, ALU.mult, ALU.add))
                dve.wait_ge(q.ln_sd, n + 1)
                c.done(nc.vector.reciprocal(rstd[:, :], mean[:, :]))
                nc.vector.tensor_tensor(sq[:, :, :], Hf, b3(rstd[:, :], D), ALU.mult).then_inc(q.ln_h, 1)

            @block.scalar
            def _(act):
                act.wait_ge(q.ln, n * 6 + 3)
                nc.scalar.activation(sq[:, :, :], k.H[:, :, 0:D], ACT.Square).then_inc(q.ln_sq, 1)
                act.wait_ge(q.ln, n * 6 + 5)
                nc.scalar.activation(mean[:, :], var[:, :], ACT.Sqrt).then_inc(q.ln_sd, 1)
                act.wait_ge(q.ln_h, n * 2 + 1)
                nc.scalar.activation(k.H[:, :, 0:D], sq[:, :, :], ACT.Relu).then_inc(q.ln_h, 1)

            @block.sync
            def _(sp):
                if write:
                    sp.wait_ge(q.ln_h, n * 2 + 2)
                    sp.wait_ge(q.ln_st, 16 * write(sp, q.ln_st))


def sum_messages(nc, k, turn, key, table, width, weighted):
    cols = width + 1 if weighted else width
    with ExitStack() as ctx:
        sb = lambda n, s, d: ctx.enter_context(nc.sbuf_tensor(tagged(nc, n), s, d))
        q = k.sems
        nth = lambda t: turn * NG + t
        use = lambda i: turn * NI + i
        rec = sb("rec", [P, U, G, 4], I32)
        hs = sb("hs", [P, U, G, width], F32)
        oh = sb("oh", [P, 2, G, P], F32)
        msg = sb("msg", [P, 2, G, cols], F32) if weighted else None
        ps = ctx.enter_context(nc.psum_tensor(tagged(nc, "ps"), [P, 2, 512], F32))
        recf = rec[:, :, :, :].bitcast(F32)
        with nc.Block() as block:

            @block.sync
            def _(sp):
                def step(i, j):
                    t = i * U + j
                    if not (isinstance(i, int) and i == 0):
                        sp.wait_ge(q.gather[j], use(i) * (16 * G))
                        sp.sem_inc(q.gate_sp, 1)
                        sp.wait_ge(q.msg if weighted else q.oh, nth(t - U + 1))
                        sp.sem_inc(q.gate_sp, 1)
                    sp.dma_start(rec[:, j, :, :], k.rec_d[key, :, ds(t * G, G), :]).then_inc(q.rec[j], 16)
                pipeline(sp, step, 0)

            @block.gpsimd
            def _(pool):
                def step(i, j):
                    t = i * U + j
                    if not (isinstance(i, int) and i == 0):
                        pool.wait_ge(q.msg if weighted else q.v, nth(t - U + 1))
                    pool.wait_ge(q.rec[j], use(i) * 16 + 16)
                    pool.sem_inc(q.gate_pool, 1)
                    for g in range(G):
                        nc.gpsimd.indirect_dma_start(
                            out=hs[:, j, g, :], out_offset=None, in_=table,
                            in_offset=bass.IndirectOffsetOnAxis(ap=rec[:, j, g, 0:1], axis=0)).then_inc(q.gather[j], 16)
                pipeline(pool, step, 0)

            @block.vector
            def _(dve):
                nc.vector.memset(k.acc[:, :, :], 0.0).then_inc(q.clear, 1)
                if weighted:
                    nc.vector.memset(msg[:, :, :, :], 1.0).then_inc(q.clear, 1)
                dve.wait_ge(q.clear, 2 * turn + (2 if weighted else 1))

                blocks = Numbers(nc, dve, k.gb[:, key, :], "block")

                def step(i, j):
                    if now := lagged(i, j, 0):
                        i0, _, t = now
                        dve.wait_ge(q.rec[j], use(i0) * 16 + 16)
                        if not (isinstance(t, int) and t < 2):
                            dve.wait_ge(q.v, nth(t - 1))
                        nc.vector.tensor_tensor(oh[:, j % 2, :, :], mid(k.iota[:, :], G),
                                                b3(recf[:, j, :, 1], P), ALU.is_equal).then_inc(q.oh, 1)
                        if weighted:
                            dve.wait_ge(q.gather[j], use(i0) * (16 * G) + 16 * G)
                            nc.vector.tensor_tensor(msg[:, j % 2, :, 0:width], hs[:, j, :, :],
                                                    b3(recf[:, j, :, 2], width), ALU.mult).then_inc(q.msg, 1)
                    if last := lagged(i, j, 1):
                        _, j1, t = last
                        b = blocks.at(j, 1)
                        a = pick(k.acc, b, slice(0, cols)).rearrange("p a c -> p (a c)")
                        dve.wait_ge(q.v, nth(t) + 1)
                        if not (isinstance(t, int) and t < 1):
                            dve.wait_ge(q.u, nth(t))
                        nc.vector.tensor_tensor(a, a, ps[:, j1 % 2, 0:cols], ALU.add).then_inc(q.u, 1)
                pipeline(dve, step, 1, numbers=blocks)

            @block.tensor
            def _(pe):
                def step(i, j):
                    t = i * U + j
                    pe.wait_ge(q.oh, nth(t) + 1)
                    if not (isinstance(t, int) and t < 2):
                        pe.wait_ge(q.u, nth(t - 1))
                    if weighted:
                        pe.wait_ge(q.msg, nth(t) + 1)
                    else:
                        pe.wait_ge(q.gather[j], use(i) * (16 * G) + 16 * G)
                    for g in range(G):
                        r = msg[:, j % 2, g, :] if weighted else hs[:, j, g, :]
                        mm = nc.tensor.matmul(ps[:, j % 2, 0:cols], oh[:, j % 2, g, :], r, start=(g == 0), stop=(g == G - 1))
                    mm.then_inc(q.v, 1)
                pipeline(pe, step, 0)


def weighted_means(nc, k, a):
    for turn, (key, table, lo) in enumerate(((0, k.tab_bwd, DH), (1, k.tab_fwd, 0))):
        sum_messages(nc, k, turn, key, table, DH, True)
        with ExitStack() as ctx:
            sem = lambda n: ctx.enter_context(nc.semaphore(tagged(nc, n)))
            s_deg = sem("s_deg")
            rdeg = ctx.enter_context(nc.sbuf_tensor(tagged(nc, "rdeg"), [P, NB], F32))
            one = ctx.enter_context(nc.sbuf_tensor(tagged(nc, "one"), [P, 1], F32))
            with nc.Block() as block:

                @block.vector
                def _(dve):
                    c = Chain(dve, s_deg)
                    c.done(nc.vector.tensor_scalar(k.deg[:, key, :], k.cnt_of(key), 1.0, None, ALU.max))
                    c.done(nc.vector.reciprocal(rdeg[:, :], k.deg[:, key, :]))
                    c.done(nc.vector.tensor_tensor(k.acc[:, :, 0:DH], k.acc[:, :, 0:DH], b3(rdeg[:, :], DH), ALU.mult))
                    c.done(nc.vector.tensor_tensor(k.X[:, :, lo:lo + DH], k.X[:, :, lo:lo + DH], k.acc[:, :, 0:DH], ALU.add))


def block_steps(eng, step, lag):
    step(0)
    with eng.Fori(1, NB) as b:
        step(b)
    for n in range(lag):
        step(NB + n)


def paired_blocks(eng, step, lag):
    for b in range(3):
        step(b, b % 2)
    with eng.Fori(1, (NB - 1) // 2) as i:
        step(i * 2 + 1, 1)
        step(i * 2 + 2, 0)
    for b in range(NB, NB + lag):
        step(b, b % 2)


def block_before(b, lag):
    if isinstance(b, int) and not 0 <= b - lag < NB:
        return None
    return (b - lag,)


def graph_conv(nc, k, a):
    layernorm(nc, k, None)
    with ExitStack() as ctx:
        sb = lambda n, s, d: ctx.enter_context(nc.sbuf_tensor(tagged(nc, n), s, d))
        sem = lambda n: ctx.enter_context(nc.semaphore(tagged(nc, n)))
        s_sd = sem("s_sd")
        s_rs = sem("s_rs")
        s_st = sem("s_st")
        root = sb("root", [P, 2, NB], F32)
        rs = sb("rs", [P, 2, NB], F32)
        with nc.Block() as block:

            @block.scalar
            def _(act):
                nc.scalar.activation(root[:, :, :], k.deg[:, :, :], ACT.Sqrt).then_inc(s_sd, 1)

            @block.vector
            def _(dve):
                dve.wait_ge(s_sd, 1)
                nc.vector.reciprocal(rs[:, :, :], root[:, :, :]).then_inc(s_rs, 1)
                dve.wait_ge(s_rs, 1)
                nc.vector.tensor_tensor(k.acc[:, :, 0:D], k.H[:, :, 0:D], b3(rs[:, 1, :], D), ALU.mult).then_inc(s_rs, 1)

            @block.sync
            def _(sp):
                sp.wait_ge(s_rs, 2)
                sp.dma_start(rows(k.tab_gc), k.acc[:, :, 0:D]).then_inc(s_st, 16)
                sp.wait_ge(s_st, 16)

        sum_messages(nc, k, 2, 0, k.tab_gc, D, False)

        s_w = sem("s_w")
        s_bias = sem("s_bias")
        s_ms = sem("s_ms")
        s_hc = sem("s_hc")
        s_t1 = sem("s_t1")
        s_mt = sem("s_mt")
        s_mm = sem("s_mm")
        s_y = sem("s_y")
        s_yc = sem("s_yc")
        s_t2 = sem("s_t2")
        s_xt = sem("s_xt")
        s_lg = sem("s_lg")
        s_l = sem("s_l")
        W = sb("W", [P, 2, 2, D], F32)
        Wg = sb("Wg", [P, 2, EXPERTS], F32)
        bias2 = sb("bias2", [1, 2, D], F32)
        bias = sb("bias", [1, D], F32)
        bg = sb("bg", [1, EXPERTS], F32)
        mh = sb("mh", [P, 2, D], F32)
        mhT = sb("mhT", [P, 4, P], F32)
        xs = sb("xs", [P, D], F32)
        xT = sb("xT", [P, 2, P], F32)
        ps = lambda n, s: ctx.enter_context(nc.psum_tensor(tagged(nc, n), s, F32))
        psT = ps("psT", [P, 4, P])
        psX = ps("psX", [P, 512])
        psU = ps("psU", [P, 4, P])
        psG = ps("psG", [P, 512])
        with nc.Block() as block:

            @block.sync
            def _(sp):
                for n, w in enumerate((a["L1_gnn_W_gc"], a["L1_gnn_W_res"])):
                    sp.dma_start(W[:, n, :, :], w.rearrange("(c p) n -> p c n", p=P)).then_inc(s_w, 16)
                sp.dma_start(Wg[:, :, :], a["L1_gnn_Wg"].rearrange("(c p) n -> p c n", p=P)).then_inc(s_w, 16)
                for n, v in enumerate((a["L1_gnn_b_gc"], a["L1_gnn_b_res"])):
                    sp.dma_start(bias2[:, n, :], v.unsqueeze(0)).then_inc(s_w, 16)
                sp.dma_start(bg[:, :], a["L1_gnn_bg"].unsqueeze(0)).then_inc(s_w, 16)

            @block.vector
            def _(dve):
                dve.wait_ge(s_w, 6 * 16)
                nc.vector.tensor_tensor(bias[:, :], bias2[:, 0, :], bias2[:, 1, :], ALU.add).then_inc(s_bias, 1)

                def step(b):
                    if not (isinstance(b, int) and b == NB):
                        if not (isinstance(b, int) and b == 0):
                            dve.wait_ge(s_t1, b)
                        nc.vector.tensor_scalar(mh[:, 0, :], pick(k.acc, b, slice(0, D)).rearrange("p a c -> p (a c)"),
                                                rs[:, 0, ds(b, 1)], None, ALU.mult).then_inc(s_ms, 1)
                        dve.wait_ge(s_mm, b + 1)
                        if not (isinstance(b, int) and b == 0):
                            dve.wait_ge(s_t2, b)
                            dve.wait_ge(s_yc, b)
                        nc.vector.tensor_copy(xs[:, :], psX[:, 0:D]).then_inc(s_y, 1)
                    if not (isinstance(b, int) and b == 0):
                        dve.wait_ge(s_lg, b)
                        nc.vector.tensor_copy(pick(k.logits, b - 1, slice(None)).rearrange("p a c -> p (a c)"),
                                              psG[:, 0:EXPERTS]).then_inc(s_l, 1)
                block_steps(dve, step, 1)

            @block.scalar
            def _(act):
                def step(b):
                    if not (isinstance(b, int) and b == NB):
                        if not (isinstance(b, int) and b == 0):
                            act.wait_ge(s_t1, b)
                            act.sem_inc(s_gate, 1)
                        nc.scalar.activation(mh[:, 1, :], pick(k.H, b, slice(0, D)).rearrange("p a c -> p (a c)"),
                                             ACT.Copy).then_inc(s_hc, 1)
                        act.wait_ge(s_t1, b + 1)
                        if not (isinstance(b, int) and b == 0):
                            act.wait_ge(s_mm, b)
                        nc.scalar.activation(mhT[:, :, :], psT[:, :, :], ACT.Copy).then_inc(s_mt, 1)
                    if not (isinstance(b, int) and b == 0):
                        act.wait_ge(s_t2, b)
                        if not (isinstance(b, int) and b == 1):
                            act.wait_ge(s_lg, b - 1)
                        nc.scalar.activation(xT[:, :, :], psU[:, 0:2, :], ACT.Copy).then_inc(s_xt, 1)
                    if not (isinstance(b, int) and b == NB):
                        act.wait_ge(s_y, b + 1)
                        act.sem_inc(s_gate, 1)
                        nc.scalar.activation(pick(k.Y, b, slice(None)).rearrange("p a c -> p (a c)"), xs[:, :],
                                             ACT.Copy).then_inc(s_yc, 1)
                s_gate = sem("s_gate")
                block_steps(act, step, 1)

            @block.tensor
            def _(pe):
                pe.wait_ge(s_w, 6 * 16)
                pe.wait_ge(s_bias, 1)

                def step(b):
                    first, end = isinstance(b, int) and b == 0, isinstance(b, int) and b == NB
                    if not end:
                        pe.wait_ge(s_ms, b + 1)
                        pe.wait_ge(s_hc, b + 1)
                        if not first:
                            pe.wait_ge(s_mt, b)
                        for n in range(4):
                            t = nc.tensor.transpose(psT[:, n, :], mh[:, n // 2, (n % 2) * P:(n % 2 + 1) * P], k.ident[:, :])
                        t.then_inc(s_t1, 1)
                    if not first:
                        pe.wait_ge(s_y, b)
                        if not (isinstance(b, int) and b == 1):
                            pe.wait_ge(s_xt, b - 1)
                        for n in range(2):
                            t = nc.tensor.transpose(psU[:, n, :], xs[:, n * P:(n + 1) * P], k.ident[:, :])
                        t.then_inc(s_t2, 1)
                    if not end:
                        pe.wait_ge(s_mt, b + 1)
                        if not first:
                            pe.wait_ge(s_y, b)
                        for n in range(4):
                            nc.tensor.matmul(psX[:, 0:D], mhT[:, n, :], W[:, n // 2, n % 2, :], start=(n == 0), stop=False)
                        nc.tensor.matmul(psX[:, 0:D], k.ones[0:1, 0:P], bias[:, :], start=False, stop=True).then_inc(s_mm, 1)
                    if not first:
                        pe.wait_ge(s_xt, b)
                        if not (isinstance(b, int) and b == 1):
                            pe.wait_ge(s_l, b - 1)
                        for n in range(2):
                            nc.tensor.matmul(psG[:, 0:EXPERTS], xT[:, n, :], Wg[:, n, :], start=(n == 0), stop=False)
                        nc.tensor.matmul(psG[:, 0:EXPERTS], k.ones[0:1, 0:P], bg[:, :], start=False, stop=True).then_inc(s_lg, 1)
                block_steps(pe, step, 1)


def route(nc, k, a):
    with ExitStack() as ctx:
        sb = lambda n, s, d=F32: ctx.enter_context(nc.sbuf_tensor(tagged(nc, n), s, d))
        sem = lambda n: ctx.enter_context(nc.semaphore(tagged(nc, n)))
        s_iota = sem("s_iota")
        s_chain = sem("s_chain")
        s_exp = sem("s_exp")
        s_pre = sem("s_pre")
        s_et = sem("s_et")
        s_etd = sem("s_etd")
        X3 = [P, NB, EXPERTS]
        enum = sb("enum", [P, EXPERTS])
        node = sb("node", [P, NB])
        valid = sb("valid", [P, NB])
        one = [sb(f"one{n}", X3) for n in range(2)]
        tmp = sb("tmp", X3)
        rest = sb("rest", X3)
        cnt = sb("cnt", X3)
        rank = sb("rank", X3)
        tots = sb("tots", X3)
        run = sb("run", [P, NB + 1, EXPERTS])
        top = sb("top", [P, 2, NB])
        idx = sb("idx", [P, 2, NB])
        ex = sb("ex", [P, 2, NB])
        ne_i = sb("ne_i", [P, EXPERTS], I32)
        ne = sb("ne", [P, EXPERTS])
        base = sb("base", [P, EXPERTS])
        tend = sb("tend", [P, EXPERTS])
        slotf = sb("slotf", [P, 2, NB])
        okf = sb("okf", [P, 2, NB])
        beyond = sb("beyond", [P, 2, NB])
        et_f = sb("et_f", [P, 1])
        et_i = sb("et_i", [P, 1], I32)
        CH = 400
        NC = NB * EXPERTS // CH
        pre = ctx.enter_context(nc.psum_tensor(tagged(nc, "pre"), [P, NC, 512], F32))
        tot = ctx.enter_context(nc.psum_tensor(tagged(nc, "tot"), [P, NC, 512], F32))
        flat = lambda t: t[:, :, :].rearrange("p b e -> p (b e)")
        with nc.Block() as block:

            @block.gpsimd
            def _(pool):
                nc.gpsimd.iota(enum[:, :], [[1, EXPERTS]], base=0, channel_multiplier=0,
                               allow_small_or_imprecise_dtypes=True).then_inc(s_iota, 1)
                nc.gpsimd.iota(node[:, :], [[P, NB]], base=0, channel_multiplier=1,
                               allow_small_or_imprecise_dtypes=True).then_inc(s_iota, 1)
                nc.gpsimd.iota(beyond[:, :, :], [[0, 2], [0, NB]], base=MT * P, channel_multiplier=1,
                               allow_small_or_imprecise_dtypes=True).then_inc(s_iota, 1)

            @block.vector
            def _(dve):
                c = Chain(dve, s_chain)
                V = nc.vector
                dve.wait_ge(s_iota, 3)
                V.memset(k.et[:, 0:U], 0)
                V.memset(k.et[:, U + P:], 0)
                c.done(V.tensor_scalar(valid[:, :], node[:, :], float(N), None, ALU.is_lt))
                cur = k.logits
                for n in range(2):
                    c.done(V.tensor_reduce(top[:, n, :], cur[:, :, :], AX.X, ALU.max))
                    c.done(V.tensor_tensor(tmp[:, :, :], cur[:, :, :], b3(top[:, n, :], EXPERTS), ALU.not_equal))
                    c.done(V.scalar_tensor_tensor(out=tmp[:, :, :], in0=tmp[:, :, :], scalar=float(EXPERTS),
                                                  in1=mid(enum[:, :], NB), op0=ALU.mult, op1=ALU.add))
                    c.done(V.tensor_reduce(idx[:, n, :], tmp[:, :, :], AX.X, ALU.min))
                    c.done(V.tensor_tensor(one[n][:, :, :], mid(enum[:, :], NB), b3(idx[:, n, :], EXPERTS), ALU.is_equal))
                    if n == 0:
                        c.done(V.scalar_tensor_tensor(out=flat(rest), in0=flat(one[0]), scalar=-BIG, in1=flat(k.logits),
                                                      op0=ALU.mult, op1=ALU.add))
                        cur = rest
                for n in range(2):
                    c.mark(V.tensor_tensor(one[n][:, :, :], one[n][:, :, :], b3(valid[:, :], EXPERTS), ALU.mult))
                dve.wait_ge(s_chain, c.n)
                c.done(V.tensor_tensor(cnt[:, :, :], one[0][:, :, :], one[1][:, :, :], ALU.add))
                V.tensor_tensor(ex[:, 0, :], top[:, 1, :], top[:, 0, :], ALU.subtract).then_inc(s_exp, 1)
                dve.wait_ge(s_exp, 2)
                c.done(V.tensor_scalar(ex[:, 0, :], ex[:, 1, :], 1.0, None, ALU.add))
                c.done(V.reciprocal(k.gate[:, 0, :], ex[:, 0, :]))
                c.done(V.tensor_tensor(k.gate[:, 1, :], ex[:, 1, :], k.gate[:, 0, :], ALU.mult))
                dve.wait_ge(s_pre, 1)
                pv = lambda t: t[:, :, 0:CH]
                sv = lambda t: flat(t).rearrange("p (n c) -> p n c", c=CH)
                c.mark(V.tensor_copy(sv(rank), pv(pre)))
                c.mark(V.tensor_copy(sv(tots), pv(tot)))
                c.done(V.memset(run[:, 0, :], 0.0))
                dve.wait_ge(s_chain, c.n)
                at = c.n
                with dve.Fori(0, NB) as b:
                    V.tensor_tensor(pick(run, b + 1, slice(None)), pick(run, b, slice(None)), pick(tots, b, slice(None)),
                                    ALU.add).then_inc(s_chain, 1)
                    dve.wait_ge(s_chain, b + at + 1)
                c.n = at + NB
                dve.wait_ge(s_chain, c.n)
                c.done(V.tensor_tensor(rank[:, :, :], rank[:, :, :], run[:, 0:NB, :], ALU.add))
                c.done(V.tensor_scalar(ne[:, :], run[:, NB, :], float(CAP), float(P - 1), ALU.min, ALU.add))
                c.done(V.tensor_copy(ne_i[:, :], ne[:, :]))
                c.done(V.tensor_scalar(ne_i[:, :], ne_i[:, :], 7, None, ALU.arith_shift_right))
                c.done(V.tensor_copy(ne[:, :], ne_i[:, :]))
                c.done(V.tensor_tensor_scan(tend[:, :], k.ones[:, 0:EXPERTS], ne[:, :], 0.0, ALU.mult, ALU.add))
                c.done(V.tensor_tensor(base[:, :], tend[:, :], ne[:, :], ALU.subtract))
                c.done(V.tensor_scalar(ne[:, :], tend[:, :], k.pcol[:, 0:1], None, ALU.is_le))
                c.done(V.tensor_reduce(et_f[:, :], ne[:, :], AX.X, ALU.add))
                V.tensor_scalar(et_i[:, :], et_f[:, :], float(EXPERTS - 1), None, ALU.min).then_inc(s_et, 1)
                c.done(V.tensor_scalar(cnt[:, :, :], rank[:, :, :], float(CAP), None, ALU.is_lt))
                c.done(V.tensor_scalar(base[:, :], base[:, :], float(P), None, ALU.mult))
                c.done(V.tensor_tensor(rank[:, :, :], rank[:, :, :], mid(base[:, :], NB), ALU.add))
                for n in range(2):
                    c.done(V.tensor_tensor(tmp[:, :, :], one[n][:, :, :], cnt[:, :, :], ALU.mult))
                    c.done(V.tensor_reduce(okf[:, n, :], tmp[:, :, :], AX.X, ALU.add))
                    c.done(V.tensor_tensor(tmp[:, :, :], tmp[:, :, :], rank[:, :, :], ALU.mult))
                    c.done(V.tensor_reduce(slotf[:, n, :], tmp[:, :, :], AX.X, ALU.add))
                c.mark(V.tensor_copy(k.slot_get[:, :, :], slotf[:, :, :].rearrange("p n b -> p b n")))
                c.done(V.tensor_tensor(k.gate[:, :, :], k.gate[:, :, :], okf[:, :, :], ALU.mult))
                c.done(V.tensor_tensor(slotf[:, :, :], slotf[:, :, :], beyond[:, :, :], ALU.add))
                c.done(V.tensor_tensor(okf[:, :, :], okf[:, :, :], beyond[:, :, :], ALU.mult))
                c.done(V.tensor_tensor(k.slot_put[:, :, :].rearrange("p b n -> p n b"), slotf[:, :, :], okf[:, :, :],
                                       ALU.subtract))

            @block.scalar
            def _(act):
                act.wait_ge(s_exp, 1)
                nc.scalar.activation(ex[:, 1, :], ex[:, 0, :], ACT.Exp).then_inc(s_exp, 1)

            @block.tensor
            def _(pe):
                pe.wait_ge(s_exp, 1)
                for n in range(NC):
                    r = flat(cnt)[:, n * CH:(n + 1) * CH]
                    nc.tensor.matmul(pre[:, n, 0:CH], k.tri[:, :], r, start=True, stop=True)
                    mm = nc.tensor.matmul(tot[:, n, 0:CH], k.ones[:, 0:P], r, start=True, stop=True)
                mm.then_inc(s_pre, 1)

            @block.sync
            def _(sp):
                sp.wait_ge(s_et, 1)
                sp.dma_start(k.et_d, et_i[:, :]).then_inc(s_etd, 16)
                sp.wait_ge(s_etd, 16)
                sp.dma_start(k.et[:, U:U + P], k.et_d.rearrange("p a -> (p a)").unsqueeze(0)).then_inc(s_etd, 16)
                sp.wait_ge(s_etd, 32)

    RING = 5
    with ExitStack() as ctx:
        sb = lambda n, s, d=F32: ctx.enter_context(nc.sbuf_tensor(tagged(nc, n), s, d))
        sem = lambda n: ctx.enter_context(nc.semaphore(tagged(nc, n)))
        s_row = [sem(f"s_row{n}") for n in range(RING)]
        s_put = [sem(f"s_put{n}") for n in range(RING)]
        s_gate = sem("s_gate")
        row = sb("row", [P, RING, D])
        to = sb("to", [P, RING, 2], I32)
        with nc.Block() as block:

            @block.vector
            def _(dve):
                with dve.Fori(0, NB // RING) as i:
                    for n in range(RING):
                        b = i * RING + n
                        dve.wait_ge(s_put[n], i * 32)
                        nc.vector.tensor_copy(row[:, n:n + 1, :], pick(k.Y, b, slice(None))).then_inc(s_row[n], 1)
                        nc.vector.tensor_copy(to[:, n:n + 1, :], pick(k.slot_put, b, slice(None))).then_inc(s_row[n], 1)

            @block.gpsimd
            def _(pool):
                with pool.Fori(0, NB // RING) as i:
                    for n in range(RING):
                        pool.wait_ge(s_row[n], i * 2 + 2)
                        pool.sem_inc(s_gate, 1)
                        for m in range(TOP_K):
                            nc.gpsimd.indirect_dma_start(
                                out=k.xbuf, out_offset=bass.IndirectOffsetOnAxis(ap=to[:, n, m:m + 1], axis=0),
                                in_=row[:, n, :], in_offset=None, bounds_check=MT * P - 1,
                                oob_is_err=False).then_inc(s_put[n], 16)
                for n in range(RING):
                    pool.wait_ge(s_put[n], NB // RING * 32)


def experts(nc, k, a):
    with ExitStack() as ctx:
        sb = lambda n, s, d=F32: ctx.enter_context(nc.sbuf_tensor(tagged(nc, n), s, d))
        sem = lambda n: ctx.enter_context(nc.semaphore(tagged(nc, n)))
        HC = HID // P
        s_b1 = sem("s_b1")
        s_b1t = sem("s_b1t")
        s_b1c = sem("s_b1c")
        s_x = [sem(f"s_x{n}") for n in range(U)]
        s_w = [sem(f"s_w{n}") for n in range(U)]
        s_bias = sem("s_bias")
        s_tx = sem("s_tx")
        s_xT = sem("s_xT")
        s_h = sem("s_h")
        s_g = sem("s_g")
        s_y = sem("s_y")
        s_ys = sem("s_ys")
        s_out = [sem(f"s_out{n}") for n in range(U)]
        s_gate = sem("s_gate")
        s_gate2 = sem("s_gate2")
        b1 = sb("b1", [EXPERTS, HID])
        b1T = sb("b1T", [P, EXPERTS, HC])
        w1 = sb("w1", [P, U, 2, HID])
        w2 = sb("w2", [P, U, HC, D])
        b2 = sb("b2", [1, U, D])
        x = sb("x", [P, U, D])
        bias = sb("bias", [P, 2, HC])
        xT = sb("xT", [P, 2, 2, P])
        h = sb("h", [P, 2, HC, P])
        y = sb("y", [P, U, D])
        ps = lambda n, s: ctx.enter_context(nc.psum_tensor(tagged(nc, n), s, F32))
        psx = ps("psx", [P, 2, 4, P])
        psh = ps("psh", [P, 2, HC, P])
        psy = ps("psy", [P, 2, 512])

        def late(t, n):
            return not (isinstance(t, int) and t < n)

        with nc.Block() as block:

            @block.sync
            def _(sp):
                sp.dma_start(b1[:, :], a["L1_gnn_b1"]).then_inc(s_b1, 16)

                tiles = Numbers(nc, sp, k.et[:, :], "expert", EXPERTS - 1)

                def step(i, n):
                    t = i * U + n
                    e = tiles.at(n, 0)
                    if late(t, U):
                        sp.wait_ge(s_h, t - U + 1)
                        sp.sem_inc(s_gate, 1)
                    sp.dma_start(x[:, n, :], k.xbuf_t[ds(t, 1), :, :].rearrange("a p c -> (a p) c")).then_inc(s_x[n], 16)
                    sp.dma_start(w1[:, n, :, :], a["L1_gnn_w1"][ds(e, 1), :, :].rearrange("a (c p) h -> p (a c) h", p=P)).then_inc(s_w[n], 16)
                    if late(t, U):
                        sp.wait_ge(s_y, t - U + 1)
                        sp.sem_inc(s_gate, 1)
                    sp.dma_start(w2[:, n, :, :], a["L1_gnn_w2"][ds(e, 1), :, :].rearrange("a (c p) h -> p (a c) h", p=P)).then_inc(s_w[n], 16)
                    sp.dma_start(b2[:, n, :], a["L1_gnn_b2"][ds(e, 1), :]).then_inc(s_w[n], 16)
                pipeline(sp, step, 0, MT, numbers=tiles)

            @block.gpsimd
            def _(pool):
                def step(i, n):
                    t = i * U + n
                    pool.wait_ge(s_ys, t + 1)
                    pool.sem_inc(s_gate2, 1)
                    pool.dma_start(k.ybuf_t[ds(t, 1), :, :].rearrange("a p c -> (a p) c"), y[:, n, :]).then_inc(s_out[n], 16)
                pipeline(pool, step, 0, MT)
                for n in range(U):
                    pool.wait_ge(s_out[n], MT // U * 16)

            @block.vector
            def _(dve):
                dve.wait_ge(s_b1t, 1)
                nc.vector.tensor_copy(b1T[:, :, :].rearrange("p e c -> p c e"), psx[:, 0, :, 0:EXPERTS]).then_inc(s_b1c, 1)
                dve.wait_ge(s_b1c, 1)
                tiles = Numbers(nc, dve, k.et[:, :], "expert", EXPERTS - 1)

                def step(i, n):
                    if now := lagged(i, n, 0, MT):
                        _, m, t = now
                        e = tiles.at(n, 0)
                        if late(t, 2):
                            dve.wait_ge(s_g, t - 1)
                        nc.vector.tensor_copy(bias[:, m % 2:m % 2 + 1, :], pick(b1T, e, slice(None))).then_inc(s_bias, 1)
                        if late(t, 2):
                            dve.wait_ge(s_h, t - 1)
                        dve.wait_ge(s_tx, t + 1)
                        nc.vector.tensor_copy(xT[:, m % 2, :, :], psx[:, m % 2, 0:2, :]).then_inc(s_xT, 1)
                    if old := lagged(i, n, 2, MT):
                        i2, m, t = old
                        dve.wait_ge(s_y, t + 1)
                        if late(t, U):
                            dve.wait_ge(s_out[m], i2 * 16)
                        nc.vector.tensor_copy(y[:, m, :], psy[:, m % 2, 0:D]).then_inc(s_ys, 1)
                pipeline(dve, step, 2, MT, numbers=tiles)

            @block.scalar
            def _(act):
                def step(i, n):
                    if last := lagged(i, n, 1, MT):
                        _, m, t = last
                        m %= 2
                        act.wait_ge(s_h, t + 1)
                        act.wait_ge(s_bias, t + 1)
                        if late(t, 2):
                            act.wait_ge(s_y, t - 1)
                        for c in range(HC):
                            g = nc.scalar.activation(h[:, m, c, :], psh[:, m, c, :], ACT.Gelu, bias=bias[:, m, c:c + 1])
                        g.then_inc(s_g, 1)
                pipeline(act, step, 1, MT)

            @block.tensor
            def _(pe):
                pe.wait_ge(s_b1, 16)
                for c in range(HC):
                    t = nc.tensor.transpose(psx[:, 0, c, 0:EXPERTS], b1[:, c * P:(c + 1) * P], k.ident[0:EXPERTS, 0:EXPERTS])
                t.then_inc(s_b1t, 1)
                pe.wait_ge(s_b1c, 1)

                def step(i, n):
                    if now := lagged(i, n, 0, MT):
                        i0, m, t = now
                        pe.wait_ge(s_x[m], i0 * 16 + 16)
                        if late(t, 2):
                            pe.wait_ge(s_xT, t - 1)
                        for c in range(2):
                            tr = nc.tensor.transpose(psx[:, m % 2, c, :], x[:, m, c * P:(c + 1) * P], k.ident[:, :])
                        tr.then_inc(s_tx, 1)
                    if last := lagged(i, n, 1, MT):
                        i1, m, t = last
                        pe.wait_ge(s_w[m], i1 * 48 + 48)
                        pe.wait_ge(s_xT, t + 1)
                        if late(t, 2):
                            pe.wait_ge(s_g, t - 1)
                        for c in range(HC):
                            for d in range(2):
                                mm = nc.tensor.matmul(psh[:, m % 2, c, :], w1[:, m, d, c * P:(c + 1) * P], xT[:, m % 2, d, :],
                                                      start=(d == 0), stop=(d == 1))
                        mm.then_inc(s_h, 1)
                    if old := lagged(i, n, 2, MT):
                        _, m, t = old
                        pe.wait_ge(s_g, t + 1)
                        if late(t, 2):
                            pe.wait_ge(s_ys, t - 1)
                        for c in range(HC):
                            nc.tensor.matmul(psy[:, m % 2, 0:D], h[:, m % 2, c, :], w2[:, m, c, :], start=(c == 0), stop=False)
                        nc.tensor.matmul(psy[:, m % 2, 0:D], k.ones[0:1, 0:P], b2[:, m, :], start=False, stop=True).then_inc(s_y, 1)
                pipeline(pe, step, 2, MT)


def combine(nc, k, a):
    RING = 5
    with ExitStack() as ctx:
        sb = lambda n, s, d=F32: ctx.enter_context(nc.sbuf_tensor(tagged(nc, n), s, d))
        sem = lambda n: ctx.enter_context(nc.semaphore(tagged(nc, n)))
        s_from = [sem(f"s_from{n}") for n in range(RING)]
        s_get = [sem(f"s_get{n}") for n in range(RING)]
        s_add = sem("s_add")
        s_gate = sem("s_gate")
        s_gb = sem("s_gb")
        s_sum = sem("s_sum")
        s_bn = sem("s_bn")
        s_sq = sem("s_sq")
        s_sd = sem("s_sd")
        row = sb("row", [P, RING, TOP_K, D])
        frm = sb("frm", [P, RING, TOP_K], I32)
        aff = sb("aff", [P, 2, D])
        mean = sb("mean", [P, D])
        var = sb("var", [P, D])
        std = sb("std", [P, D])
        ps = ctx.enter_context(nc.psum_tensor(tagged(nc, "ps"), [P, 2, 512], F32))
        Yf = k.Y[:, :, :]
        with nc.Block() as block:

            @block.sync
            def _(sp):
                for n, v in enumerate((a["L1_gnn_gamma"], a["L1_gnn_beta"])):
                    sp.dma_start(aff[:, n, :], v.partition_broadcast(P)).then_inc(s_gb, 16)

            @block.gpsimd
            def _(pool):
                with pool.Fori(0, NB // RING) as i:
                    for n in range(RING):
                        pool.wait_ge(s_from[n], i + 1)
                        pool.sem_inc(s_gate, 1)
                        for m in range(TOP_K):
                            nc.gpsimd.indirect_dma_start(
                                out=row[:, n, m, :], out_offset=None, in_=k.ybuf,
                                in_offset=bass.IndirectOffsetOnAxis(ap=frm[:, n, m:m + 1], axis=0)).then_inc(s_get[n], 16)

            @block.vector
            def _(dve):
                V = nc.vector
                with dve.Fori(0, NB // RING) as i:
                    for n in range(RING):
                        dve.wait_ge(s_add, i * (2 * RING))
                        V.tensor_copy(frm[:, n:n + 1, :], pick(k.slot_get, i * RING + n, slice(None))).then_inc(s_from[n], 1)
                    for n in range(RING):
                        b = i * RING + n
                        y = pick(k.Y, b, slice(None)).rearrange("p a c -> p (a c)")
                        dve.wait_ge(s_get[n], i * 32 + 32)
                        for m in range(TOP_K):
                            V.scalar_tensor_tensor(out=y, in0=row[:, n, m, :], scalar=k.gate[:, m, ds(b, 1)], in1=y,
                                                   op0=ALU.mult, op1=ALU.add).then_inc(s_add, 1)
                            dve.wait_ge(s_add, i * (2 * RING) + (2 * n + m + 1))
                c = Chain(dve, s_bn)
                dve.wait_ge(s_sum, 1)
                c.done(V.tensor_scalar(mean[:, :], ps[:, 0, 0:D], 1.0 / N, None, ALU.mult))
                c.done(V.tensor_tensor(Yf, Yf, mid(mean[:, :], NB), ALU.subtract))
                dve.wait_ge(s_sum, 2)
                c.done(V.tensor_scalar(var[:, :], ps[:, 1, 0:D], 1.0 / N, BN_EPS, ALU.mult, ALU.add))
                dve.wait_ge(s_sd, 1)
                c.done(V.reciprocal(var[:, :], std[:, :]))
                dve.wait_ge(s_gb, 32)
                c.done(V.tensor_tensor(var[:, :], var[:, :], aff[:, 0, :], ALU.mult))
                c.done(V.tensor_tensor(Yf, Yf, mid(var[:, :], NB), ALU.mult))
                c.done(V.tensor_tensor(Yf, Yf, mid(aff[:, 1, :], NB), ALU.add))
                c.done(V.tensor_tensor(k.X[:, :, :], k.X[:, :, :], Yf, ALU.add))

            @block.scalar
            def _(act):
                act.wait_ge(s_bn, 2)
                nc.scalar.activation(k.acc[:, :, 0:D], Yf, ACT.Square).then_inc(s_sq, 1)
                act.wait_ge(s_bn, 3)
                nc.scalar.activation(std[:, :], var[:, :], ACT.Sqrt).then_inc(s_sd, 1)

            @block.tensor
            def _(pe):
                for n, (src, wait) in enumerate(((k.Y, (s_add, 2 * NB)), (k.acc, (s_sq, 1)))):
                    pe.wait_ge(*wait)
                    nc.tensor.matmul(ps[:, n, 0:D], k.ones[0:LAST, 0:P], src[0:LAST, NB - 1, 0:D], start=True, stop=False)
                    for b in range(NB - 1):
                        mm = nc.tensor.matmul(ps[:, n, 0:D], k.ones[:, 0:P], src[:, b, 0:D], start=False, stop=(b == NB - 2))
                    mm.then_inc(s_sum, 1)


def attention_by_angle(nc, k, a):
    layernorm(nc, k, None)
    with ExitStack() as ctx:
        sb = lambda n, s, d=F32: ctx.enter_context(nc.sbuf_tensor(tagged(nc, n), s, d))
        sem = lambda n: ctx.enter_context(nc.semaphore(tagged(nc, n)))
        q = k.sems
        HN = sb("HN", [P, NB, D])
        betas = sb("betas", [P, L2_LAYERS])
        peak = sb("peak", [P, NB])
        ss = sb("ss", [P, NB])
        rn = sb("rn", [P, NB])
        rnb = sb("rnb", [P, NB])
        s_beta = sem("s_beta")
        s_node = sem("s_node")
        s_sq = sem("s_sq")
        s_tab = sem("s_tab")
        s_end = sem("s_end")
        s_g = sem("s_g")
        s_l = sem("s_l")
        s_mx = sem("s_mx")
        s_p = sem("s_p")
        rec = sb("rec", [P, U, G, 4], I32)
        hs = sb("hs", [P, U, G, W_AGNN])
        oh = sb("oh", [P, U, G, P], BF16)
        ohT = sb("ohT", [P, U, G, P])
        neg = sb("neg", [P, U, G * P])
        prod = sb("prod", [P, G, D])
        cand = sb("cand", [P, 2, G * P])
        lg = sb("lg", [P, 2, G])
        tt = sb("tt", [P, 2, G])
        below = sb("below", [P, 2, G])
        ex = sb("ex", [P, 2, G])
        pr = sb("pr", [P, 2, G, P])
        mt = sb("mt", [P, 2])
        mn = sb("mn", [P, 2])
        df = sb("df", [P, 2])
        rs = sb("rs", [P, U])
        ps = lambda n, s, d=F32: ctx.enter_context(nc.psum_tensor(tagged(nc, n), s, d))
        psT = ps("psT", [P, G * P * 2], BF16)[:, 0:G * P]
        psG = ps("psG", [P, 2, G, D])
        psL = ps("psL", [P, G * P])
        psQ = ps("psQ", [P, 512])
        psV = ps("psV", [P, 512])
        recf = rec[:, :, :, :].bitcast(F32)
        cols = D + 2
        with nc.Block() as block:

            @block.sync
            def _(sp):
                sp.dma_start(betas[:, :], a["L2_gnn_betas"].partition_broadcast(P)).then_inc(s_beta, 16)
                sp.wait_ge(s_beta, 16)

            @block.vector
            def _(dve):
                nc.vector.memset(k.H[:, :, D + 1:W_AGNN], 1.0)

        with nc.Fori(0, L2_LAYERS) as layer:
            with nc.Block() as block:

                @block.scalar
                def _(act):
                    nc.scalar.activation(HN[:, :, :], k.H[:, :, 0:D], ACT.Square).then_inc(s_sq, 1)
                    act.wait_ge(s_node, layer * 5 + 2)
                    nc.scalar.activation(rn[:, :], ss[:, :], ACT.Sqrt).then_inc(s_sq, 1)

                @block.vector
                def _(dve):
                    c = Chain(dve, s_node, layer * 5)
                    nc.vector.memset(k.acc[:, :, :], 0.0)
                    nc.vector.memset(peak[:, :], -BIG)
                    dve.wait_ge(s_sq, layer * 2 + 1)
                    c.done(nc.vector.tensor_reduce(ss[:, :], HN[:, :, :], AX.X, ALU.add))
                    c.done(nc.vector.tensor_scalar(ss[:, :], ss[:, :], 1e-16, None, ALU.add))
                    dve.wait_ge(s_sq, layer * 2 + 2)
                    c.done(nc.vector.reciprocal(k.H[:, :, D], rn[:, :]))
                    c.done(nc.vector.tensor_scalar(rnb[:, :], k.H[:, :, D], betas[:, ds(layer, 1)], None, ALU.mult))
                    c.mark(nc.vector.tensor_tensor(HN[:, :, :], k.H[:, :, 0:D], b3(rnb[:, :], D), ALU.mult))

                @block.sync
                def _(sp):
                    sp.wait_ge(s_node, layer * 5 + 3)
                    sp.dma_start(rows(k.tab_agnn), k.H[:, :, 0:W_AGNN]).then_inc(s_tab, 16)
                    sp.wait_ge(s_tab, layer * 16 + 16)
                    sp.sem_inc(q.gate_sp, 1)

            with nc.Block() as block:
                nth = lambda t: layer * NG + (3 * NG + t)
                use = lambda i: layer * NI + (3 * NI + i)
                own = flow = lambda t: layer * NG + t

                @block.sync
                def _(sp):
                    def step(i, j):
                        t = i * U + j
                        if not (isinstance(i, int) and i == 0):
                            sp.wait_ge(q.gather[j], use(i) * (16 * G))
                            sp.sem_inc(q.gate_sp, 1)
                            sp.wait_ge(q.oh, nth(t - U + 1))
                            sp.sem_inc(q.gate_sp, 1)
                        sp.dma_start(rec[:, j, :, :], k.rec_d[0, :, ds(t * G, G), :]).then_inc(q.rec[j], 16)
                    pipeline(sp, step, 0)

                @block.gpsimd
                def _(pool):
                    def step(i, j):
                        t = i * U + j
                        if not (isinstance(i, int) and i == 0):
                            pool.wait_ge(q.v, nth(t - U + 1))
                        pool.wait_ge(q.rec[j], use(i) * 16 + 16)
                        pool.sem_inc(q.gate_pool, 1)
                        for g in range(G):
                            nc.gpsimd.indirect_dma_start(
                                out=hs[:, j, g, :], out_offset=None, in_=k.tab_agnn,
                                in_offset=bass.IndirectOffsetOnAxis(ap=rec[:, j, g, 0:1], axis=0)).then_inc(q.gather[j], 16)
                    pipeline(pool, step, 0)

                @block.vector
                def _(dve):
                    V = nc.vector
                    blocks = Numbers(nc, dve, k.gb[:, 0, :], "block")

                    def step(i, j):
                        now, mid_, old, add = lagged(i, j, 0), lagged(i, j, 2), lagged(i, j, 3), lagged(i, j, 4)
                        if mid_:
                            i2, j2, t2 = mid_
                            h2 = j2 % 2
                            at = pick(peak, blocks.at(j, 2))
                            dve.wait_ge(q.gather[j2], use(i2) * (16 * G) + 16 * G)
                            dve.wait_ge(s_g, own(t2) + 1)
                            for g in range(G):
                                ins = V.tensor_tensor_reduce(prod[:, g, :], psG[:, h2, g, :], hs[:, j2, g, 0:D], hs[:, j2, g, D:D + 1],
                                                             0.0, ALU.mult, ALU.add, lg[:, h2, g:g + 1])
                            ins.then_inc(s_l, 1)
                        if old:
                            _, j3, t3 = old
                            h3 = j3 % 2
                            dve.wait_ge(q.q, flow(t3) + 1)
                            V.tensor_tensor(tt[:, h3, :], lg[:, h3, :], psQ[:, 0:G], ALU.subtract).then_inc(q.tt, 1)
                        if old:
                            dve.wait_ge(q.tt, flow(t3) + 1)
                            V.tensor_scalar(below[:, h3, :], tt[:, h3, :], 0.0, None, ALU.min).then_inc(q.min, 1)
                        if now:
                            i0, _, t = now
                            dve.wait_ge(q.rec[j], use(i0) * 16 + 16)
                            if not (isinstance(t, int) and t < U):
                                dve.wait_ge(s_p, own(t - U + 1))
                            V.tensor_tensor(oh[:, j, :, :], mid(k.iota[:, :], G), b3(recf[:, j, :, 1], P),
                                            ALU.is_equal).then_inc(q.oh, 1)
                        if add:
                            _, j4, t4 = add
                            acc = pick(k.acc, blocks.at(j, 4), slice(0, cols)).rearrange("p a c -> p (a c)")
                            dve.wait_ge(q.v, nth(t4) + 1)
                            dve.wait_ge(q.rs, flow(t4) + 1)
                            if not (isinstance(t4, int) and t4 < 1):
                                dve.wait_ge(q.u, nth(t4))
                            V.scalar_tensor_tensor(out=acc, in0=acc, scalar=rs[:, j4:j4 + 1], in1=psV[:, 0:cols],
                                                   op0=ALU.mult, op1=ALU.add).then_inc(q.u, 1)
                        if mid_:
                            dve.wait_ge(q.b, flow(t2) + 1)
                            dve.wait_ge(q.ev, flow(t2) + 1)
                            dve.sem_inc(q.gate_dve, 1)
                            V.tensor_tensor_reduce(cand[:, h2, :], psL[:, :], neg[:, j2, :], 1.0, -BIG, ALU.add, ALU.max,
                                                   mt[:, h2:h2 + 1]).then_inc(s_mx, 1)

                        def weighted(*tiles):
                            if old:
                                dve.wait_ge(q.e, flow(t3) + 1)
                                for g in tiles:
                                    ins = V.tensor_scalar(pr[:, h3, g, :], oh[:, j3, g, :], ex[:, h3, g:g + 1], None, ALU.mult)
                                if g == G - 1:
                                    ins.then_inc(s_p, 1)
                        weighted(0)
                        if mid_:
                            dve.wait_ge(s_mx, own(t2) * 2 + 1)
                            V.tensor_tensor(mn[:, h2:h2 + 1], at, mt[:, h2:h2 + 1], ALU.max).then_inc(q.m, 1)
                        weighted(1)
                        if mid_:
                            dve.wait_ge(q.m, flow(t2) + 1)
                            V.tensor_tensor(df[:, h2:h2 + 1], at, mn[:, h2:h2 + 1], ALU.subtract).then_inc(q.df, 1)
                        weighted(2, 3)
                        if mid_:
                            dve.wait_ge(q.df, flow(t2) + 1)
                            dve.sem_inc(q.gate_dve, 1)
                            V.tensor_copy(at, mn[:, h2:h2 + 1]).then_inc(s_mx, 1)
                    pipeline(dve, step, 4, numbers=blocks)

                @block.scalar
                def _(act):
                    def step(i, j):
                        now, mid_, old = lagged(i, j, 0), lagged(i, j, 2), lagged(i, j, 3)
                        if old:
                            _, j3, t3 = old
                            h = j3 % 2
                            act.wait_ge(q.min, flow(t3) + 1)
                            if not (isinstance(t3, int) and t3 < 2):
                                act.wait_ge(s_p, own(t3 - 1))
                            nc.scalar.activation(ex[:, h, :], below[:, h, :], ACT.Exp).then_inc(q.e, 1)
                        if now:
                            _, _, t = now
                            act.wait_ge(q.t, flow(t) + 1)
                            if not (isinstance(t, int) and t < U):
                                act.wait_ge(q.q, flow(t - U + 1))
                            nc.scalar.activation(ohT[:, j, :, :].rearrange("p g e -> p (g e)"), psT[:, :], ACT.Copy)
                            nc.scalar.activation(neg[:, j, :], psT[:, :], ACT.Copy, bias=-BIG, scale=BIG).then_inc(q.ev, 1)
                        if mid_:
                            _, j2, t2 = mid_
                            act.wait_ge(q.df, flow(t2) + 1)
                            if not (isinstance(t2, int) and t2 < U):
                                act.wait_ge(q.u, nth(t2 - U + 1))
                            nc.scalar.activation(rs[:, j2:j2 + 1], df[:, j2 % 2:j2 % 2 + 1], ACT.Exp).then_inc(q.rs, 1)
                    pipeline(act, step, 3)

                @block.tensor
                def _(pe):
                    blocks = Numbers(nc, pe, k.gb[:, 0, :], "block")

                    def step(i, j):
                        now, last, mid_, old = (lagged(i, j, n) for n in range(4))
                        if mid_:
                            _, j2, t2 = mid_
                            h2 = j2 % 2
                            pe.wait_ge(s_l, own(t2) + 1)
                            if not (isinstance(t2, int) and t2 < 1):
                                pe.wait_ge(q.m, flow(t2))
                            for g in range(G):
                                mm = nc.tensor.transpose(psL[:, g * P:(g + 1) * P], lg[:, h2, g:g + 1].to_broadcast([P, P]), k.ident[:, :])
                            mm.then_inc(q.b, 1)
                        if last:
                            _, j1, t1 = last
                            b = blocks.at(j, 1)
                            pe.wait_ge(q.ev, flow(t1) + 1)
                            if not (isinstance(t1, int) and t1 < 2):
                                pe.wait_ge(s_l, own(t1 - 1))
                            for g in range(G):
                                mm = nc.tensor.matmul(psG[:, j1 % 2, g, :], ohT[:, j1, g, :],
                                                      pick(HN, b, slice(None)).rearrange("p a c -> p (a c)"), start=True, stop=True)
                            mm.then_inc(s_g, 1)
                        if now:
                            _, _, t = now
                            pe.wait_ge(q.oh, nth(t) + 1)
                            if not (isinstance(t, int) and t < 1):
                                pe.wait_ge(q.ev, flow(t))
                            for g in range(G):
                                mm = nc.tensor.transpose(psT[:, g * P:(g + 1) * P], oh[:, j, g, :], k.identb[:, :])
                            mm.then_inc(q.t, 1)
                        if mid_:
                            pe.wait_ge(q.m, flow(t2) + 1)
                            if not (isinstance(t2, int) and t2 < 1):
                                pe.wait_ge(q.tt, flow(t2))
                            for g in range(G):
                                mm = nc.tensor.matmul(psQ[:, g:g + 1], ohT[:, j2, g, :], mn[:, h2:h2 + 1], start=True, stop=True)
                            mm.then_inc(q.q, 1)
                        if old:
                            _, j3, t3 = old
                            pe.wait_ge(s_p, own(t3) + 1)
                            if not (isinstance(t3, int) and t3 < 1):
                                pe.wait_ge(q.u, nth(t3))
                            for g in range(G):
                                mm = nc.tensor.matmul(psV[:, 0:cols], pr[:, j3 % 2, g, :], hs[:, j3, g, 0:cols],
                                                      start=(g == 0), stop=(g == G - 1))
                            mm.then_inc(q.v, 1)
                    pipeline(pe, step, 3, numbers=blocks)

            with nc.Block() as block:

                @block.vector
                def _(dve):
                    c = Chain(dve, s_end, layer * 4)
                    V = nc.vector
                    c.done(V.tensor_scalar(ss[:, :], k.acc[:, :, D + 1], 1e-16, None, ALU.add))
                    c.done(V.reciprocal(rn[:, :], ss[:, :]))
                    c.done(V.tensor_tensor(HN[:, :, :], k.acc[:, :, 0:D], b3(rn[:, :], D), ALU.mult))
                    c.mark(V.tensor_scalar(k.H[:, :, 0:D], HN[:, :, :], 0.0, None, ALU.max))

        s_x = sem("s_x")
        with nc.Block() as block:

            @block.vector
            def _(dve):
                nc.vector.tensor_tensor(k.X[:, :, :], k.X[:, :, :], k.H[:, :, 0:D], ALU.add).then_inc(s_x, 1)
                dve.wait_ge(s_x, 1)


def graph_attention(nc, k, a):
    layernorm(nc, k, None)
    with ExitStack() as ctx:
        sb = lambda n, s, d=F32: ctx.enter_context(nc.sbuf_tensor(tagged(nc, n), s, d))
        sem = lambda n: ctx.enter_context(nc.semaphore(tagged(nc, n)))
        q = k.sems
        W = sb("W", [P, L3_LAYERS, 2, W_GAT + HEADS])
        att = sb("att", [P, 2, L3_LAYERS, D])
        prod = sb("prod", [P, 2, 2, D])
        last_b = sb("last_b", [P, D])
        bcol = sb("bcol", [P, L3_LAYERS, 2])
        bnow = sb("bnow", [P, 2])
        sp_ = sb("sp", [P, NB, 2, HEADS])
        smax = sb("smax", [P, NB, HEADS])
        part = sb("part", [P, NB, HEADS])
        heads = sb("heads", [P, 1], I32)
        headf = sb("headf", [P, 1])
        sel = sb("sel", [P, HEADS, P], BF16)
        sd, peak = sp_[:, :, 0, :], sp_[:, :, 1, :]
        den = sb("den", [P, NB, HEADS])
        node = sb("node", [P, NB])
        loop = sb("loop", [P, NB])
        noloop = sb("noloop", [P, NB])
        nrm = sb("nrm", [P, NB])
        rt = sb("rt", [P, NB])
        s_w = sem("s_w")
        s_first = sem("s_first")
        s_end = sem("s_end")
        H4 = k.H[:, :, 0:W_GAT].rearrange("p b (h c) -> p b h c", h=HEADS)
        A4 = k.acc[:, :, :].rearrange("p b (h c) -> p b h c", h=HEADS)
        with nc.Block() as block:

            @block.sync
            def _(sp):
                for n in range(L3_LAYERS):
                    w, src, dst, b = (a[f"L3_gnn_{v}{n + 1}"] for v in ("W", "a_src", "a_dst", "b"))
                    for c in range(2):
                        sp.dma_start(W[:, n, c, 0:W_GAT].rearrange("p (h c) -> p h c", h=HEADS)[:, :, 0:C_HEAD],
                                     w[c * P:(c + 1) * P, :].rearrange("p (h c) -> p h c", h=HEADS)).then_inc(s_w, 16)
                        if n < L3_LAYERS - 1:
                            sp.dma_start(bcol[:, n + 1, c:c + 1], b[c * P:(c + 1) * P].unsqueeze(1)).then_inc(s_w, 16)
                    sp.dma_start(att[:, 0, n, :], src.rearrange("h c -> (h c)").partition_broadcast(P)).then_inc(s_w, 16)
                    sp.dma_start(att[:, 1, n, :], dst.rearrange("h c -> (h c)").partition_broadcast(P)).then_inc(s_w, 16)
                sp.dma_start(last_b[:, :], b.partition_broadcast(P)).then_inc(s_w, 16)

            @block.vector
            def _(dve):
                V = nc.vector
                c = Chain(dve, s_first, 1)
                dve.wait_ge(s_first, 1)
                c.mark(V.memset(bcol[:, 0, :], 0.0))
                c.mark(V.memset(den[:, :, :], 1.0))
                c.mark(V.tensor_copy(A4[:, :, :, 0:C_HEAD], k.H[:, :, 0:D].rearrange("p b (h c) -> p b h c", h=HEADS)))
                c.mark(V.tensor_scalar(loop[:, :], node[:, :], float(LOOPS), None, ALU.is_lt))
                c.done(V.tensor_copy(heads[:, :], k.pcol[:, :]))
                dve.wait_ge(s_first, 1 + c.n)
                c.done(V.tensor_scalar(noloop[:, :], loop[:, :], 1.0, BIG, ALU.subtract, ALU.mult))
                c.done(V.tensor_scalar(heads[:, :], heads[:, :], HEADS - 1, None, ALU.bitwise_and))
                c.done(V.tensor_copy(headf[:, :], heads[:, :]))
                for m in range(HEADS):
                    V.tensor_scalar(sel[:, m, :], headf[:, 0:1].to_broadcast([P, P]), float(m), None, ALU.is_equal)
                dve.wait_ge(s_w, (4 * L3_LAYERS + 2 * (L3_LAYERS - 1) + 1) * 16)
                for n in range(L3_LAYERS):
                    for v in range(2):
                        for r in range(2):
                            c.mark(V.tensor_tensor(prod[:, v, r, :].rearrange("p (h c) -> p h c", h=HEADS),
                                                   W[:, n, r, 0:W_GAT].rearrange("p (h c) -> p h c", h=HEADS)[:, :, 0:C_HEAD],
                                                   att[:, v, n, :].rearrange("p (h c) -> p h c", h=HEADS), ALU.mult))
                    dve.wait_ge(s_first, 1 + c.n)
                    c.mark(V.tensor_reduce(W[:, n, :, 0:W_GAT].rearrange("p r (h c) -> p r h c", h=HEADS)[:, :, :, C_HEAD],
                                           prod[:, 0, :, :].rearrange("p r (h c) -> p r h c", h=HEADS), AX.X, ALU.add))
                    c.mark(V.tensor_reduce(W[:, n, :, W_GAT:],
                                           prod[:, 1, :, :].rearrange("p r (h c) -> p r h c", h=HEADS), AX.X, ALU.add))
                    dve.wait_ge(s_first, 1 + c.n)

            @block.gpsimd
            def _(pool):
                nc.gpsimd.iota(node[:, :], [[P, NB]], base=0, channel_multiplier=1,
                               allow_small_or_imprecise_dtypes=True).then_inc(s_first, 1)

        s_xs = sem("s_xs")
        s_tr = sem("s_tr")
        s_xT = sem("s_xT")
        s_mm = sem("s_mm")
        s_h = sem("s_h")
        s_bn = sem("s_bn")
        s_node = sem("s_node")
        s_tab = sem("s_tab")
        s_mx = sem("s_mx")
        s_lt = sem("s_lt")
        s_lg = sem("s_lg")
        s_st = sem("s_st")
        s_of = sem("s_of")
        s_away = sem("s_away")
        with nc.Fori(0, L3_LAYERS) as layer:
            with ExitStack() as node:
                psT = node.enter_context(nc.psum_tensor(tagged(nc, "psT"), [P, 2, 512], F32))
                psH = node.enter_context(nc.psum_tensor(tagged(nc, "psH"), [P, 2, 512], F32))
                xs = node.enter_context(nc.sbuf_tensor(tagged(nc, "xs"), [P, 2, D], F32))
                xT = node.enter_context(nc.sbuf_tensor(tagged(nc, "xT"), [P, 2, 2, P], F32))
                with nc.Block() as block:
                    nth = lambda b: layer * NB + b
                    row = lambda v, b, n: pick(v, b, slice(0, n)).rearrange("p a c -> p (a c)")

                    @block.vector
                    def _(dve):
                        V = nc.vector
                        V.tensor_copy(bnow[:, :], bcol[:, ds(layer, 1), :].rearrange("p a c -> p (a c)")).then_inc(s_bn, 1)

                        def step(b, slot):
                            if now := block_before(b, 0):
                                b0, = now
                                if not (isinstance(b0, int) and b0 < 2):
                                    dve.wait_ge(s_tr, nth(b0 - 1))
                                V.tensor_tensor(xs[:, slot, :].rearrange("p (h c) -> p h c", h=HEADS),
                                                row(k.acc, b0, W_GAT).rearrange("p (h c) -> p h c", h=HEADS)[:, :, 0:C_HEAD],
                                                b3(row(den, b0, HEADS), C_HEAD), ALU.mult).then_inc(s_xs, 1)
                            if old := block_before(b, 2):
                                b2, = old
                                dve.wait_ge(s_mm, nth(b2) + 1)
                                V.tensor_copy(row(k.H, b2, W_GAT), psH[:, slot, 0:W_GAT])
                                V.tensor_copy(pick(sp_, b2, 0, slice(None)).rearrange("p a c -> p (a c)"),
                                              psH[:, slot, W_GAT:W_GAT + HEADS]).then_inc(s_h, 1)
                        paired_blocks(dve, step, 2)
                        dve.wait_ge(s_h, nth(NB))
                        c = Chain(dve, s_node, layer * 11)
                        parts = k.H[:, :, W_GAT:W_ROW].bitcast(BF16)
                        left = H4[:, :, :, C_HEAD]
                        for n in range(3):
                            piece = parts[:, :, n * HEADS:(n + 1) * HEADS]
                            c.done(V.tensor_copy(piece, left))
                            if n < 2:
                                c.done(V.tensor_tensor(part[:, :, :], left, piece, ALU.subtract))
                            left = part[:, :, :]
                        c.mark(V.tensor_tensor(k.acc[:, 0:LB, :], k.H[:, 0:LB, 0:W_GAT], b3(loop[:, 0:LB], W_GAT), ALU.mult))
                        c.done(V.tensor_tensor(den[:, :, :], H4[:, :, :, C_HEAD], b3(loop[:, :], HEADS), ALU.mult))
                        c.mark(V.tensor_tensor(smax[:, :, :], den[:, :, :], b3(noloop[:, :], HEADS), ALU.add))
                        c.done(V.tensor_copy(A4[:, 0:LB, :, C_HEAD], b3(loop[:, 0:LB], HEADS)))
                        c.done(V.tensor_tensor(den[:, :, :], smax[:, :, :], sd, ALU.add))
                        c.mark(V.scalar_tensor_tensor(out=peak, in0=den[:, :, :],
                                                      scalar=NEG_SLOPE, in1=den[:, :, :], op0=ALU.mult, op1=ALU.max))

                    @block.gpsimd
                    def _(pool):
                        pool.wait_ge(s_xs, nth(NB))
                        pool.sem_inc(q.gate_pool, 1)
                        nc.gpsimd.memset(k.acc[:, LB:, :], 0.0)

                    @block.scalar
                    def _(act):
                        act.wait_ge(s_bn, layer + 1)

                        def step(b, slot):
                            act.wait_ge(s_tr, nth(b) + 1)
                            if not (isinstance(b, int) and b < 2):
                                act.wait_ge(s_mm, nth(b - 1))
                            for c in range(2):
                                ins = nc.scalar.activation(xT[:, slot, c, :], psT[:, slot, c * P:(c + 1) * P], ACT.Relu, bias=bnow[:, c:c + 1])
                            ins.then_inc(s_xT, 1)
                        paired_blocks(act, step, 0)

                    @block.tensor
                    def _(pe):
                        def step(b, slot):
                            if now := block_before(b, 0):
                                b0, = now
                                pe.wait_ge(s_xs, nth(b0) + 1)
                                if not (isinstance(b0, int) and b0 < 2):
                                    pe.wait_ge(s_xT, nth(b0 - 1))
                                for n in range(2):
                                    mm = nc.tensor.transpose(psT[:, slot, n * P:(n + 1) * P], xs[:, slot, n * P:(n + 1) * P], k.ident[:, :])
                                mm.then_inc(s_tr, 1)
                            if last := block_before(b, 1):
                                b1, = last
                                pe.wait_ge(s_xT, nth(b1) + 1)
                                if not (isinstance(b1, int) and b1 < 2):
                                    pe.wait_ge(s_h, nth(b1 - 1))
                                for n in range(2):
                                    mm = nc.tensor.matmul(psH[:, 1 - slot, 0:W_GAT + HEADS], xT[:, 1 - slot, n, :],
                                                          W[:, ds(layer, 1), n, :].rearrange("p a c -> p (a c)"), start=(n == 0), stop=(n == 1))
                                mm.then_inc(s_mm, 1)
                        paired_blocks(pe, step, 1)

                    @block.sync
                    def _(sp):
                        sp.wait_ge(s_node, layer * 11 + 5)
                        sp.dma_start(rows(k.tab_gat), k.H[:, :, :]).then_inc(s_tab, 16)
                        sp.wait_ge(s_tab, layer * 16 + 16)
                        sp.sem_inc(q.gate_sp, 1)

            with ExitStack() as grp:
                sb = lambda n, s, d=F32: grp.enter_context(nc.sbuf_tensor(tagged(nc, n), s, d))
                rec = sb("rec", [P, U, G, 4], I32)
                hs = sb("hs", [P, U, G, W_ROW])
                oh = sb("oh", [P, U, G, P], BF16)
                away = sb("away", [P, G, P], BF16)
                ohf = sb("ohf", [P, 2, G, P])
                ohT = sb("ohT", [P, 2, G, P])
                neg = sb("neg", [P, 2, G * P])
                sT = sb("sT", [PARTS, 2, G * P], BF16)
                cand = sb("cand", [P, HEADS, G * P])
                msg = sb("msg", [P, 2, G, W_GAT])
                mt = sb("mt", [P, 2, HEADS])
                xx = sb("xx", [P, 2, HEADS])
                top = sb("top", [P, 2, HEADS])
                df = sb("df", [P, 2, HEADS])
                rs = sb("rs", [P, U, HEADS])
                t1 = sb("t1", [P, 2, G * HEADS])
                t2_ = sb("t2_", [P, 2, G * HEADS])
                t3 = sb("t3", [P, 2, G * HEADS])
                below = sb("below", [P, 2, G * HEADS])
                ps = lambda n, s, d=F32: grp.enter_context(nc.psum_tensor(tagged(nc, n), s, d))
                psT = ps("psT", [P, 2, G * P], BF16)
                psL = ps("psL", [P, HEADS, G * P])
                psQ = ps("psQ", [P, 512])
                psV = ps("psV", [P, 2, 512])
                recf = rec[:, :, :, :].bitcast(F32)
                hsb = hs[:, :, :, :].bitcast(BF16)
                with nc.Block() as block:
                    PASSES = 3 + L2_LAYERS
                    nth = lambda t: layer * NG + (PASSES * NG + t)
                    use = lambda i: layer * NI + (PASSES * NI + i)
                    own = lambda t: layer * NG + t
                    flow = lambda t: layer * NG + (L2_LAYERS * NG + t)
                    spread = lambda t: layer * (NG * HEADS) + (L2_LAYERS * NG + t * HEADS)
                    by_head = lambda t: layer * (NG * HEADS) + t * HEADS

                    @block.sync
                    def _(sp):
                        def step(i, j):
                            t = i * U + j
                            if not (isinstance(i, int) and i == 0):
                                sp.wait_ge(q.gather[j], use(i) * (16 * G))
                                sp.sem_inc(q.gate_sp, 1)
                                sp.wait_ge(q.oh, nth(t - U + 1))
                                sp.sem_inc(q.gate_sp, 1)
                            sp.dma_start(rec[:, j, :, :], k.rec_d[0, :, ds(t * G, G), :]).then_inc(q.rec[j], 16)
                        pipeline(sp, step, 0)

                    @block.gpsimd
                    def _(pool):
                        def step(i, j):
                            t = i * U + j
                            if not (isinstance(i, int) and i == 0):
                                pool.wait_ge(q.msg3, own(t - U + 1))
                            pool.wait_ge(q.rec[j], use(i) * 16 + 16)
                            pool.sem_inc(q.gate_pool, 1)
                            for g in range(G):
                                nc.gpsimd.indirect_dma_start(
                                    out=hs[:, j, g, :], out_offset=None, in_=k.tab_gat,
                                    in_offset=bass.IndirectOffsetOnAxis(ap=rec[:, j, g, 0:1], axis=0)).then_inc(q.gather[j], 16)
                        pipeline(pool, step, 0)

                    @block.vector
                    def _(dve):
                        V = nc.vector
                        blocks = Numbers(nc, dve, k.gb[:, 0, :], "block")

                        def step(i, j):
                            mid_, old, add = lagged(i, j, 2), lagged(i, j, 3), lagged(i, j, 4)
                            if old:
                                _, j3, t = old
                                h = j3 % 2
                                hrow = hs[:, j3, :, 0:W_GAT].rearrange("p g (h c) -> p g h c", h=HEADS)
                                hmsg = msg[:, h, :, :].rearrange("p g (h c) -> p g h c", h=HEADS)
                                q3 = psQ[:, 0:G * 2 * HEADS].rearrange("p (g k h) -> p g k h", k=2, h=HEADS)
                                g3 = lambda v: v[:, h, :].rearrange("p (g h) -> p g h", h=HEADS)
                            if mid_:
                                _, j2, t2 = mid_
                                h2 = j2 % 2
                                b = blocks.at(j, 2)
                                at = lambda v: pick(v, b, slice(None)).rearrange("p a h -> p (a h)")
                            if add:
                                _, j4, t4 = add
                                b4 = blocks.at(j, 4)

                            def head(m):
                                if mid_:
                                    dve.wait_ge(q.b, spread(t2) + (m + 1))
                                    if m == 0:
                                        dve.wait_ge(q.ev, flow(t2) + 1)
                                        if not (isinstance(t2, int) and t2 < 1):
                                            dve.wait_ge(s_lt, by_head(t2))
                                    dve.sem_inc(q.gate_dve, 1)
                                    V.tensor_tensor_reduce(cand[:, m, :], psL[:, m, :], neg[:, h2, :], 1.0, -BIG, ALU.add, ALU.max,
                                                           mt[:, h2, m:m + 1]).then_inc(s_lt, 1)

                            head(0)
                            head(1)
                            if old:
                                dve.wait_ge(q.q, flow(t) + 1)
                                V.tensor_tensor(g3(t1), hrow[:, :, :, C_HEAD], q3[:, :, 0, :], ALU.add).then_inc(s_lg, 1)
                            head(2)
                            if old:
                                dve.wait_ge(s_lg, own(t) * 2 + 1)
                                V.scalar_tensor_tensor(out=t2_[:, h, :], in0=t1[:, h, :], scalar=NEG_SLOPE, in1=t1[:, h, :],
                                                       op0=ALU.mult, op1=ALU.max).then_inc(s_lg, 1)
                            head(3)
                            if old:
                                dve.wait_ge(s_lg, own(t) * 2 + 2)
                                V.tensor_tensor(g3(t3), g3(t2_), q3[:, :, 1, :], ALU.subtract).then_inc(q.tt, 1)
                            if mid_:
                                dve.wait_ge(s_lt, by_head(t2) + HEADS)
                                V.tensor_tensor(at(smax), at(smax), mt[:, h2, :], ALU.max).then_inc(s_mx, 1)
                            if old:
                                dve.wait_ge(q.tt, flow(t) + 1)
                                V.tensor_scalar(below[:, h, :], t3[:, h, :], 0.0, None, ALU.min).then_inc(q.min, 1)
                            if mid_:
                                dve.wait_ge(s_mx, own(t2) * 3 + 1)
                                V.tensor_tensor(xx[:, h2, :], at(smax), at(sd), ALU.add).then_inc(s_mx, 1)

                            def messages(tiles):
                                n = tiles.stop - tiles.start
                                return V.tensor_tensor(hmsg[:, tiles, :, 0:C_HEAD], hrow[:, tiles, :, 0:C_HEAD],
                                                       hmsg[:, tiles, :, C_HEAD].unsqueeze(3).to_broadcast([P, n, HEADS, C_HEAD]), ALU.mult)
                            if old:
                                dve.wait_ge(q.e, flow(t) + 1)
                                messages(slice(0, 2))
                            if mid_:
                                dve.wait_ge(s_mx, own(t2) * 3 + 2)
                                V.scalar_tensor_tensor(out=top[:, h2, :], in0=xx[:, h2, :], scalar=NEG_SLOPE, in1=xx[:, h2, :],
                                                       op0=ALU.mult, op1=ALU.max).then_inc(s_mx, 1)
                            if old:
                                messages(slice(2, G)).then_inc(q.msg3, 1)
                            if mid_:
                                dve.wait_ge(s_mx, own(t2) * 3 + 3)
                                if not (isinstance(t2, int) and t2 < 2):
                                    dve.wait_ge(q.rs, flow(t2 - 1))
                                V.tensor_tensor(df[:, h2, :], at(peak), top[:, h2, :], ALU.subtract).then_inc(q.df, 1)
                                dve.wait_ge(q.df, flow(t2) + 1)
                                if not (isinstance(t2, int) and t2 < 1):
                                    dve.wait_ge(q.q, flow(t2))
                                dve.sem_inc(q.gate_dve, 1)
                                V.tensor_copy(at(peak), top[:, h2, :]).then_inc(q.m, 1)
                            if add:
                                dve.wait_ge(q.rs, flow(t4) + 1)
                                dve.wait_ge(q.v, nth(t4) + 1)
                                if not (isinstance(t4, int) and t4 < 1):
                                    dve.wait_ge(q.u, nth(t4))
                                for m in range(HEADS):
                                    acc = pick(k.acc, b4, slice(m * CH1, m * CH1 + CH1)).rearrange("p a c -> p (a c)")
                                    ins = V.scalar_tensor_tensor(out=acc, in0=acc, scalar=rs[:, j4, m:m + 1],
                                                                 in1=psV[:, j4 % 2, m * CH1:m * CH1 + CH1], op0=ALU.mult, op1=ALU.add)
                                ins.then_inc(q.u, 1)
                        pipeline(dve, step, 4, numbers=blocks)

                    @block.scalar
                    def _(act):
                        def step(i, j):
                            now, last, mid_, old = (lagged(i, j, n) for n in range(4))
                            if last:
                                _, j1, t1_ = last
                                h = j1 % 2
                                act.wait_ge(q.t, flow(t1_) + 1)
                                if not (isinstance(t1_, int) and t1_ < 2):
                                    act.wait_ge(q.q, flow(t1_ - 1))
                                nc.scalar.activation(sT[:, h, :], psT[0:PARTS, 1, :], ACT.Copy).then_inc(s_st, 1)
                                nc.scalar.activation(ohT[:, h, :, :].rearrange("p g e -> p (g e)"), psT[:, 0, :], ACT.Copy)
                                nc.scalar.activation(neg[:, h, :], psT[:, 0, :], ACT.Copy, bias=-BIG, scale=BIG).then_inc(q.ev, 1)
                            if old:
                                _, j3, t = old
                                h = j3 % 2
                                if not (isinstance(t, int) and t < 2):
                                    act.wait_ge(q.v, nth(t - 1))
                                act.wait_ge(q.min, flow(t) + 1)
                                nc.scalar.activation(msg[:, h, :, :].rearrange("p g (h c) -> p (g h) c", h=HEADS)[:, :, C_HEAD],
                                                     below[:, h, :], ACT.Exp).then_inc(q.e, 1)
                                act.wait_ge(q.oh, nth(t) + 1)
                                nc.scalar.activation(ohf[:, h, :, :].rearrange("p g e -> p (g e)"),
                                                     oh[:, j3, :, :].rearrange("p g e -> p (g e)"), ACT.Copy).then_inc(s_of, 1)
                            if now:
                                i0, _, t0 = now
                                act.wait_ge(q.rec[j], use(i0) * 16 + 16)
                                if not (isinstance(t0, int) and t0 < 1):
                                    act.wait_ge(q.oh, nth(t0))
                                if not (isinstance(t0, int) and t0 < U):
                                    act.wait_ge(s_of, own(t0 - U + 1))
                                for g in range(G):
                                    ins = nc.scalar.activation(away[:, g, :], k.iota[:, :], ACT.Abs, bias=recf[:, j, g, 1:2], scale=-1.0)
                                ins.then_inc(s_away, 1)
                                act.wait_ge(s_away, own(t0) + 1)
                                nc.scalar.activation(oh[:, j, :, :].rearrange("p g e -> p (g e)"), away[:, :, :].rearrange("p g e -> p (g e)"),
                                                     ACT.Relu, bias=1.0, scale=-1.0).then_inc(q.oh, 1)
                            if mid_:
                                _, j2, t2 = mid_
                                act.wait_ge(q.df, flow(t2) + 1)
                                if not (isinstance(t2, int) and t2 < U):
                                    act.wait_ge(q.u, nth(t2 - U + 1))
                                nc.scalar.activation(rs[:, j2, :], df[:, j2 % 2, :], ACT.Exp).then_inc(q.rs, 1)
                        pipeline(act, step, 3)

                    @block.tensor
                    def _(pe):
                        blocks = Numbers(nc, pe, k.gb[:, 0, :], "block")

                        def step(i, j):
                            last, mid_, add = lagged(i, j, 1), lagged(i, j, 2), lagged(i, j, 4)
                            if mid_:
                                _, j2, t2 = mid_
                                b = blocks.at(j, 2)
                            if last:
                                i1, j1, t1_ = last
                                h1 = j1 % 2
                                pe.wait_ge(q.oh, nth(t1_) + 1)
                                pe.wait_ge(q.gather[j1], use(i1) * (16 * G) + 16 * G)
                                if not (isinstance(t1_, int) and t1_ < 1):
                                    pe.wait_ge(q.ev, flow(t1_))
                                for g in range(G):
                                    nc.tensor.transpose(psT[0:PARTS, 1, g * P:(g + 1) * P], hsb[:, j1, g, 2 * W_GAT:], k.identb[:, :])
                                    mm = nc.tensor.transpose(psT[:, 0, g * P:(g + 1) * P], oh[:, j1, g, :], k.identb[:, :])
                                mm.then_inc(q.t, 1)
                            if add:
                                _, j4, t4 = add
                                h4 = j4 % 2
                                pe.wait_ge(q.msg3, own(t4) + 1)
                                pe.wait_ge(s_of, own(t4) + 1)
                                if not (isinstance(t4, int) and t4 < 2):
                                    pe.wait_ge(q.u, nth(t4 - 1))
                                for g in range(G):
                                    mm = nc.tensor.matmul(psV[:, h4, 0:W_GAT], ohf[:, h4, g, :], msg[:, h4, g, :],
                                                          start=(g == 0), stop=(g == G - 1))
                                mm.then_inc(q.v, 1)
                            if last:
                                pe.wait_ge(s_st, own(t1_) + 1)
                                for m in range(HEADS):
                                    if not (isinstance(t1_, int) and t1_ < 1):
                                        pe.wait_ge(s_lt, by_head(t1_ - 1) + (m + 1))
                                    nc.tensor.matmul(psL[:, m, :], sel[0:PARTS, m, :], sT[:, h1, :], start=True, stop=True).then_inc(q.b, 1)
                            if mid_:
                                pe.wait_ge(q.m, flow(t2) + 1)
                                if not (isinstance(t2, int) and t2 < 1):
                                    pe.wait_ge(q.tt, flow(t2))
                                for g in range(G):
                                    mm = nc.tensor.matmul(psQ[:, g * 8:(g + 1) * 8], ohT[:, j2 % 2, g, :],
                                                          pick(sp_, b, slice(None), slice(None)).rearrange("p a k h -> p (a k h)"),
                                                          start=True, stop=True)
                                mm.then_inc(q.q, 1)
                        pipeline(pe, step, 4, numbers=blocks)

            with nc.Block() as block:

                @block.vector
                def _(dve):
                    c = Chain(dve, s_end, layer * 2)
                    c.done(nc.vector.tensor_scalar(smax[:, :, :], A4[:, :, :, C_HEAD], 1e-30, None, ALU.max))
                    c.mark(nc.vector.reciprocal(den[:, :, :], smax[:, :, :]))

        F = k.H[:, :, 0:D]
        s_norm = sem("s_norm")
        s_sq = sem("s_sq")
        with nc.Block() as block:

            @block.scalar
            def _(act):
                act.wait_ge(s_norm, 2)
                nc.scalar.activation(k.acc[:, :, 0:D], F, ACT.Square).then_inc(s_sq, 1)
                act.wait_ge(s_norm, 3)
                nc.scalar.activation(rt[:, :], nrm[:, :], ACT.Sqrt).then_inc(s_sq, 1)

            @block.vector
            def _(dve):
                V = nc.vector
                c = Chain(dve, s_norm)
                F4 = F.rearrange("p b (h c) -> p b h c", h=HEADS)
                for m in range(HEADS):
                    ins = V.tensor_tensor(F4[:, :, m, :], A4[:, :, m, 0:C_HEAD], b3(den[:, :, m], C_HEAD), ALU.mult)
                c.done(ins)
                c.done(V.tensor_tensor(F, F, mid(last_b[:, :], NB), ALU.add))
                dve.wait_ge(s_sq, 1)
                c.done(V.tensor_reduce(nrm[:, :], k.acc[:, :, 0:D], AX.X, ALU.add))
                dve.wait_ge(s_sq, 2)
                c.done(V.tensor_scalar(nrm[:, :], rt[:, :], 1e-12, None, ALU.max))
                c.done(V.reciprocal(rt[:, :], nrm[:, :]))
                c.done(V.tensor_tensor(F, F, b3(rt[:, :], D), ALU.mult))
                c.done(V.tensor_tensor(k.X[:, :, :], k.X[:, :, :], F, ALU.add))


def build(nc, a, stop=99):
    with ExitStack() as ctx:
        sb = lambda n, s, d: ctx.enter_context(nc.sbuf_tensor(tagged(nc, n), s, d))
        k = Shared()
        k.X = sb("X", [P, NB, D], F32)
        k.H = sb("H", [P, NB, W_ROW], F32)
        k.acc = sb("acc", [P, NB, W_AGNN], F32)
        k.iota = sb("iota", [P, P], F32)
        k.pcol = sb("pcol", [P, 1], F32)
        k.ident = sb("ident", [P, P], F32)
        k.identb = sb("identb", [P, P], BF16)
        k.tri = sb("tri", [P, P], F32)
        k.ones = sb("ones", [P, D], F32)
        k.zero = sb("zero", [P, 1], F32)
        k.deg = sb("deg", [P, 2, NB], F32)
        k.gb = sb("gb", [1, 2, P + 2 * U], I32)
        k.cnt_of = lambda key: k.acc[:, :, DH]
        k.rec_d = nc.dram_tensor("rec_d", (2, P, T, 4), I32).ap()
        k.rec_rows = k.rec_d.rearrange("k p t c -> (k p t) c")
        k.gb_d = nc.dram_tensor("gb_d", (2, P, 1), I32).ap()
        k.tab_fwd = nc.dram_tensor("tab_fwd", (NP, DH), F32).ap()
        k.tab_bwd = nc.dram_tensor("tab_bwd", (NP, DH), F32).ap()
        k.tab_gc = nc.dram_tensor("tab_gc", (NP, D), F32).ap()
        k.tab_agnn = nc.dram_tensor("tab_agnn", (NP, W_AGNN), F32).ap()
        k.tab_gat = nc.dram_tensor("tab_gat", (NP, W_ROW), F32).ap()
        k.xbuf = nc.dram_tensor("xbuf", (MT * P, D), F32).ap()
        k.xbuf_t = k.xbuf.rearrange("(t p) c -> t p c", p=P)
        k.ybuf = nc.dram_tensor("ybuf", (MT * P, D), F32).ap()
        k.ybuf_t = k.ybuf.rearrange("(t p) c -> t p c", p=P)
        k.et_d = nc.dram_tensor("et_d", (P, 1), I32).ap()
        sem = lambda n: ctx.enter_context(nc.semaphore(n))
        q = k.sems = Shared()
        q.rec = [sem(f"s_rec{j}") for j in range(U)]
        q.gather = [sem(f"s_gather{j}") for j in range(U)]
        q.oh = sem("s_oh")
        q.v = sem("s_v")
        q.u = sem("s_u")
        q.msg = sem("s_msg")
        q.clear = sem("s_clear_acc")
        q.t = sem("s_t")
        q.ev = sem("s_ev")
        q.b = sem("s_b")
        q.m = sem("s_m")
        q.df = sem("s_df")
        q.rs = sem("s_rs")
        q.q = sem("s_q")
        q.tt = sem("s_tt")
        q.min = sem("s_min")
        q.e = sem("s_e")
        q.msg3 = sem("s_msg3")
        q.ln = sem("s_ln")
        q.ln_sq = sem("s_ln_sq")
        q.ln_sd = sem("s_ln_sd")
        q.ln_h = sem("s_ln_h")
        q.ln_st = sem("s_ln_st")
        q.gate_sp = sem("s_gate_sp")
        q.gate_pool = sem("s_gate_pool")
        q.gate_dve = sem("s_gate_dve")
        k.norms = 0
        with ExitStack() as early:
            k.keys = early.enter_context(nc.sbuf_tensor(tagged(nc, "keys"), [P, 2, J], I32))
            k.wts = early.enter_context(nc.sbuf_tensor(tagged(nc, "wts"), [P, J], F32))
            load_inputs(nc, k, a)
            sort_edges(nc, k)

        def write_halves(sp, s):
            sp.dma_start(rows(k.tab_fwd), k.H[:, :, 0:DH]).then_inc(s, 16)
            sp.dma_start(rows(k.tab_bwd), k.H[:, :, DH:D]).then_inc(s, 16)
            return 2
        layernorm(nc, k, write_halves)
        weighted_means(nc, k, a)
        if stop > 1:
            with ExitStack() as moe:
                msb = lambda n, s, d: moe.enter_context(nc.sbuf_tensor(n, s, d))
                k.Y = msb("Y", [P, NB, D], F32)
                k.gate = msb("gate", [P, TOP_K, NB], F32)
                k.slot_put = msb("slot_put", [P, NB, TOP_K], I32)
                k.slot_get = msb("slot_get", [P, NB, TOP_K], I32)
                k.et = msb("et", [1, P + 2 * U], I32)
                with nc.sbuf_tensor("logits", [P, NB, EXPERTS], F32) as logits:
                    k.logits = logits
                    graph_conv(nc, k, a)
                    route(nc, k, a)
                experts(nc, k, a)
                combine(nc, k, a)
        if stop > 2:
            attention_by_angle(nc, k, a)
        if stop > 3:
            graph_attention(nc, k, a)
        store(nc, k, a)


def store(nc, k, a):
    with ExitStack() as ctx:
        s_out = ctx.enter_context(nc.semaphore(tagged(nc, "s_out")))
        with nc.Block() as block:

            @block.sync
            def _(sp):
                sp.dma_start(rows(a["out"][0:(NB - 1) * P, :]), k.X[:, 0:NB - 1, :]).then_inc(s_out, 16)
                sp.dma_start(a["out"][(NB - 1) * P:N, :], k.X[0:LAST, NB - 1, :]).then_inc(s_out, 16)
                sp.wait_ge(s_out, 32)


_INS = ["x", "src", "dst", "edge_weight"] + ["L1_gnn_" + n for n in (
    "W_gc", "b_gc", "W_res", "b_res", "Wg", "bg", "w1", "b1", "w2", "b2", "gamma", "beta")] + ["L2_gnn_betas"] + [
    "L3_gnn_" + n + str(i) for i in (1, 2, 3) for n in ("W", "a_src", "a_dst", "b")]


def kernel(**inputs):
    import numpy as np
    import concourse.bacc as bacc
    from concourse.bass_utils import run_bass_kernel_spmd

    nc = bacc.Bacc("TRN2", target_bir_lowering=False, num_devices=1)
    arrays, a = {}, {}
    for name in _INS:
        v = np.ascontiguousarray(inputs[name])
        arrays["in_" + name] = v
        a[name] = nc.dram_tensor("in_" + name, v.shape, mybir.dt.from_np(v.dtype), kind="ExternalInput").ap()
    a["out"] = nc.dram_tensor("out", (N, D), F32, kind="ExternalOutput").ap()
    build(nc, a)
    r = run_bass_kernel_spmd(nc, [arrays], core_ids=[0])
    return r.results[0]["out"]
```
